# Optimizing a Trainium2 kernel written in Bass

```python
import numpy as np
import jax
import jax.numpy as jnp

def _softmax(x, axis=-1):
    return jax.nn.softmax(x, axis=axis)

def _gelu(x):
    return jax.nn.gelu(x, approximate=True)

def _silu(x):
    return jax.nn.silu(x)

def _sigmoid(x):
    return jax.nn.sigmoid(x)

def _layernorm(x, axis=-1, eps=1e-05):
    m = jnp.mean(x, axis=axis, keepdims=True)
    v = jnp.var(x, axis=axis, keepdims=True)
    return (x - m) / jnp.sqrt(v + eps)

def _scatter_add(tgt, idx, src, axis=0):
    return tgt.at[idx].add(src)

def _segment_sum(src, seg, n):
    return jax.ops.segment_sum(src, seg, n)
kernel_name = 'mk_pixart_resid_d2_seqx_r4_528a12'

def setup_inputs(seed: int=0):
    np.random.seed(seed)
    _w = jnp.asarray

    def _rec_inputs():
        import jax
        import jax.numpy as jnp
        _rk = jax.random.key(seed)
        x = 7.22e-05 + 1 * jax.random.normal(jax.random.fold_in(_rk, 1), (4, 512, 256), jnp.float32)
        _lenS = 512 - jax.random.randint(jax.random.fold_in(_rk, 7), (4,), 0, max(1, 512 // 4) + 1, jnp.int32)
        _lenS2 = 64 - jax.random.randint(jax.random.fold_in(_rk, 8), (4,), 0, max(1, 64 // 4) + 1, jnp.int32)
        _ctx_1024P = jax.random.normal(jax.random.fold_in(_rk, 11), (4, 16, 256), jnp.float32)
        _ctx_1024c = jax.random.dirichlet(jax.random.fold_in(_rk, 511), 0.3 * jnp.ones((16,), jnp.float32), (4, 64))
        _ctx_1024t = jnp.einsum('bsk,bkd->bsd', _ctx_1024c, _ctx_1024P)
        _ctx_1024t = _ctx_1024t * jax.lax.rsqrt(jnp.mean(jnp.square(_ctx_1024t)) + 1e-12) * 0.953939
        ctx_1024 = 4.13588e-05 + 0.999923 * (_ctx_1024t + 0.3 * jax.random.normal(jax.random.fold_in(_rk, 611), (4, 64, 256), jnp.float32))
        condB_tau = jax.random.uniform(jax.random.fold_in(_rk, 12), (4,), jnp.float32, 0.0, 1.45372)
        fside_BxS2_0 = 0.0088954 + 1.00633 * jax.random.normal(jax.random.fold_in(_rk, 13), (4, 64), jnp.float32)
        return (x, ctx_1024, condB_tau, fside_BxS2_0)
    x, ctx_1024, condB_tau, fside_BxS2_0 = _rec_inputs()

    def _L0_xcond_setup():
        import jax, jax.numpy as jnp
        import numpy as np
        D_MODEL = 256
        N_HEADS = 16
        key = jax.random.key(seed)
        ks = jax.random.split(key, 16)
        B, L, S, D = (4, 512, 512, D_MODEL)
        inp = {'q': jax.random.normal(ks[0], (B, L, D), jnp.float32), 'k': jax.random.normal(ks[1], (B, S, D), jnp.float32), 'v': jax.random.normal(ks[2], (B, S, D), jnp.float32), 'tau': jax.random.uniform(ks[3], (B, 1), jnp.float32, 0.5, 1.5), 'delta': jax.random.normal(ks[4], (B, S), jnp.float32)}
        s = 1.0 / np.sqrt(D)
        inp['Wq'] = jax.random.normal(ks[5], (D, D), jnp.float32) * s
        inp['bq'] = jnp.zeros((D,), jnp.float32)
        inp['Wk'] = jax.random.normal(ks[6], (D, D), jnp.float32) * s
        inp['bk'] = jnp.zeros((D,), jnp.float32)
        inp['Wv'] = jax.random.normal(ks[7], (D, D), jnp.float32) * s
        inp['bv'] = jnp.zeros((D,), jnp.float32)
        inp['Wo'] = jax.random.normal(ks[8], (D, D), jnp.float32) * s
        inp['bo'] = jnp.zeros((D,), jnp.float32)
        return inp
    _L0_xcond_all = _L0_xcond_setup()
    _L0_xcond_in = {k: v for k, v in _L0_xcond_all.items() if k in ('Wq', 'bq', 'Wk', 'bk', 'Wv', 'bv', 'Wo', 'bo')}
    del _L0_xcond_all

    def _L0_ffn_setup():
        import jax, jax.numpy as jnp
        import numpy as np
        DIM = 256

        def _reference_tuple_inner(x, W_r, W_k, W_v, mu_r, mu_k):
            B, T, C = x.shape
            x_prev = jnp.concatenate([jnp.zeros((B, 1, C), x.dtype), x[:, :-1, :]], axis=1)
            xr = mu_r * x + (1.0 - mu_r) * x_prev
            xk = mu_k * x + (1.0 - mu_k) * x_prev
            r = jax.nn.sigmoid(jnp.einsum('btc,dc->btd', xr, W_r))
            k = jnp.einsum('btc,dc->btd', xk, W_k)
            k_act = jnp.square(jax.nn.relu(k))
            out = r * jnp.einsum('btc,dc->btd', k_act, W_v)
            new_state = x[:, -1, :]
            return (out, new_state)
        key = jax.random.key(seed)
        ks = jax.random.split(key, 6)
        B, T, C = (8, 512, DIM)
        x = jax.random.normal(ks[0], (B, T, C), dtype=jnp.float32)
        s = 1.0 / np.sqrt(C)
        W_r = jax.random.uniform(ks[1], (C, C), jnp.float32, -s, s)
        W_k = jax.random.uniform(ks[2], (C, C), jnp.float32, -s, s)
        W_v = jax.random.uniform(ks[3], (C, C), jnp.float32, -s, s)
        mu_r = jax.random.uniform(ks[4], (C,), jnp.float32)
        mu_k = jax.random.uniform(ks[5], (C,), jnp.float32)
        return {'x': x, 'W_r': W_r, 'W_k': W_k, 'W_v': W_v, 'mu_r': mu_r, 'mu_k': mu_k}
    _L0_ffn_all = _L0_ffn_setup()
    _L0_ffn_in = {k: v for k, v in _L0_ffn_all.items() if k in ('W_r', 'W_k', 'W_v', 'mu_r', 'mu_k')}
    del _L0_ffn_all

    def _L1_xcond_setup():
        import jax, jax.numpy as jnp
        import numpy as np
        B, S, D, H = (2, 512, 256, 16)
        DK = D // H

        def _split_heads(x):
            b, s, _ = x.shape
            return x.reshape(b, s, H, DK).transpose(0, 2, 1, 3)
        key = jax.random.key(seed)
        ks = jax.random.split(key, 14)
        inp = {'query': jax.random.normal(ks[0], (B, S, D), jnp.float32), 'key': jax.random.normal(ks[1], (B, S, D), jnp.float32), 'value': jax.random.normal(ks[2], (B, S, D), jnp.float32), 'tau': jax.random.uniform(ks[3], (B, 1), jnp.float32, 0.5, 1.5), 'delta': jax.random.normal(ks[4], (B, S), jnp.float32)}
        sc = 1.0 / np.sqrt(D)
        for i, name in enumerate(['q', 'k', 'v', 'o']):
            inp[f'W{name}'] = jax.random.normal(ks[5 + 2 * i], (D, D), jnp.float32) * sc
            inp[f'b{name}'] = jax.random.normal(ks[6 + 2 * i], (D,), jnp.float32) * 0.01
        return inp
    _L1_xcond_all = _L1_xcond_setup()
    _L1_xcond_in = {k: v for k, v in _L1_xcond_all.items() if k in ('Wq', 'bq', 'Wk', 'bk', 'Wv', 'bv', 'Wo', 'bo')}
    del _L1_xcond_all

    def _L1_ffn_setup():
        import jax, jax.numpy as jnp
        import numpy as np
        MODEL_DIM = 256
        FF_DIM = 1024
        NUM_EXPERTS = 8
        TOP_K = 2
        BATCH, SEQ = (4, 256)

        def _moe_forward(x, W1, b1, W2, b2, Wr, br):
            B, S, D = x.shape
            T = B * S
            xf = x.reshape(T, D)
            logits = xf @ Wr + br
            probs = jax.nn.softmax(logits, axis=-1)
            topw, topi = jax.lax.top_k(probs, TOP_K)
            topw = jax.nn.softmax(topw, axis=-1)
            comb = jnp.zeros((T, NUM_EXPERTS), dtype=xf.dtype)
            comb = comb.at[jnp.arange(T)[:, None], topi].add(topw)
            h = jax.nn.gelu(jnp.einsum('td,edf->etf', xf, W1) + b1[:, None, :], approximate=False)
            eo = jnp.einsum('etf,efd->etd', h, W2) + b2[:, None, :]
            out = jnp.einsum('etd,te->td', eo, comb)
            return out.reshape(B, S, D)
        key = jax.random.key(seed)
        ks = jax.random.split(key, 8)
        s_d = 1.0 / np.sqrt(MODEL_DIM)
        s_f = 1.0 / np.sqrt(FF_DIM)
        return {'x': jax.random.normal(ks[0], (BATCH, SEQ, MODEL_DIM), dtype=jnp.float32), 'W1': jax.random.uniform(ks[1], (NUM_EXPERTS, MODEL_DIM, FF_DIM), jnp.float32, -s_d, s_d), 'b1': jax.random.uniform(ks[2], (NUM_EXPERTS, FF_DIM), jnp.float32, -s_d, s_d), 'W2': jax.random.uniform(ks[3], (NUM_EXPERTS, FF_DIM, MODEL_DIM), jnp.float32, -s_f, s_f), 'b2': jax.random.uniform(ks[4], (NUM_EXPERTS, MODEL_DIM), jnp.float32, -s_f, s_f), 'Wr': jax.random.uniform(ks[5], (MODEL_DIM, NUM_EXPERTS), jnp.float32, -s_d, s_d), 'br': jax.random.uniform(ks[6], (NUM_EXPERTS,), jnp.float32, -s_d, s_d)}
    _L1_ffn_all = _L1_ffn_setup()
    _L1_ffn_in = {k: v for k, v in _L1_ffn_all.items() if k in ('W1', 'b1', 'W2', 'b2', 'Wr', 'br')}
    del _L1_ffn_all
    return {'x': x, 'ctx_1024': ctx_1024, 'condB_tau': condB_tau, 'fside_BxS2_0': fside_BxS2_0, 'L0_xcond_Wq': _L0_xcond_in['Wq'], 'L0_xcond_bq': _L0_xcond_in['bq'], 'L0_xcond_Wk': _L0_xcond_in['Wk'], 'L0_xcond_bk': _L0_xcond_in['bk'], 'L0_xcond_Wv': _L0_xcond_in['Wv'], 'L0_xcond_bv': _L0_xcond_in['bv'], 'L0_xcond_Wo': _L0_xcond_in['Wo'], 'L0_xcond_bo': _L0_xcond_in['bo'], 'L0_ffn_W_r': _L0_ffn_in['W_r'], 'L0_ffn_W_k': _L0_ffn_in['W_k'], 'L0_ffn_W_v': _L0_ffn_in['W_v'], 'L0_ffn_mu_r': _L0_ffn_in['mu_r'], 'L0_ffn_mu_k': _L0_ffn_in['mu_k'], 'L1_xcond_Wq': _L1_xcond_in['Wq'], 'L1_xcond_bq': _L1_xcond_in['bq'], 'L1_xcond_Wk': _L1_xcond_in['Wk'], 'L1_xcond_bk': _L1_xcond_in['bk'], 'L1_xcond_Wv': _L1_xcond_in['Wv'], 'L1_xcond_bv': _L1_xcond_in['bv'], 'L1_xcond_Wo': _L1_xcond_in['Wo'], 'L1_xcond_bo': _L1_xcond_in['bo'], 'L1_ffn_W1': _L1_ffn_in['W1'], 'L1_ffn_b1': _L1_ffn_in['b1'], 'L1_ffn_W2': _L1_ffn_in['W2'], 'L1_ffn_b2': _L1_ffn_in['b2'], 'L1_ffn_Wr': _L1_ffn_in['Wr'], 'L1_ffn_br': _L1_ffn_in['br']}

def reference(x, ctx_1024, condB_tau, fside_BxS2_0, L0_xcond_Wq, L0_xcond_bq, L0_xcond_Wk, L0_xcond_bk, L0_xcond_Wv, L0_xcond_bv, L0_xcond_Wo, L0_xcond_bo, L0_ffn_W_r, L0_ffn_W_k, L0_ffn_W_v, L0_ffn_mu_r, L0_ffn_mu_k, L1_xcond_Wq, L1_xcond_bq, L1_xcond_Wk, L1_xcond_bk, L1_xcond_Wv, L1_xcond_bv, L1_xcond_Wo, L1_xcond_bo, L1_ffn_W1, L1_ffn_b1, L1_ffn_W2, L1_ffn_b2, L1_ffn_Wr, L1_ffn_br):
    import jax
    import jax.numpy as jnp

    def _L0_xcond_ref(q, k, v, tau, delta, Wq, bq, Wk, bk, Wv, bv, Wo, bo):
        import jax, jax.numpy as jnp
        import numpy as np
        D_MODEL = 256
        N_HEADS = 16
        B, L, D = q.shape
        S = k.shape[1]
        H = N_HEADS
        E = D // H
        qh = (q @ Wq.T + bq).reshape(B, L, H, E)
        kh = (k @ Wk.T + bk).reshape(B, S, H, E)
        vh = (v @ Wv.T + bv).reshape(B, S, H, E)
        scale = 1.0 / np.sqrt(E).astype(np.float32)
        scores = jnp.einsum('blhe,bshe->bhls', qh, kh)
        scores = scores * tau[:, None, None, :] + delta[:, None, None, :]
        a = jax.nn.softmax(scale * scores, axis=-1)
        out = jnp.einsum('bhls,bshd->blhd', a, vh).reshape(B, L, D)
        return out @ Wo.T + bo

    def _L0_ffn_ref(x, W_r, W_k, W_v, mu_r, mu_k):
        import jax, jax.numpy as jnp
        import numpy as np
        DIM = 256

        def _reference_tuple_inner(x, W_r, W_k, W_v, mu_r, mu_k):
            B, T, C = x.shape
            x_prev = jnp.concatenate([jnp.zeros((B, 1, C), x.dtype), x[:, :-1, :]], axis=1)
            xr = mu_r * x + (1.0 - mu_r) * x_prev
            xk = mu_k * x + (1.0 - mu_k) * x_prev
            r = jax.nn.sigmoid(jnp.einsum('btc,dc->btd', xr, W_r))
            k = jnp.einsum('btc,dc->btd', xk, W_k)
            k_act = jnp.square(jax.nn.relu(k))
            out = r * jnp.einsum('btc,dc->btd', k_act, W_v)
            new_state = x[:, -1, :]
            return (out, new_state)
        return _reference_tuple_inner(x, W_r, W_k, W_v, mu_r, mu_k)[0]

    def _L1_xcond_ref(query, key, value, tau, delta, Wq, bq, Wk, bk, Wv, bv, Wo, bo):
        import jax, jax.numpy as jnp
        import numpy as np
        B, S, D, H = (2, 512, 256, 16)
        DK = D // H

        def _split_heads(x):
            b, s, _ = x.shape
            return x.reshape(b, s, H, DK).transpose(0, 2, 1, 3)
        q = _split_heads(query @ Wq.T + bq)
        k = _split_heads(key @ Wk.T + bk)
        v = _split_heads(value @ Wv.T + bv)
        scores = jnp.einsum('bhqd,bhkd->bhqk', q, k)
        scores = scores * tau[:, :, None, None] + delta[:, None, None, :]
        scores = scores / jnp.sqrt(jnp.asarray(DK, scores.dtype))
        p_attn = jax.nn.softmax(scores, axis=-1)
        x = jnp.einsum('bhqk,bhkd->bhqd', p_attn, v)
        x = x.transpose(0, 2, 1, 3).reshape(query.shape[0], -1, H * DK)
        return x @ Wo.T + bo

    def _L1_ffn_ref(x, W1, b1, W2, b2, Wr, br):
        import jax, jax.numpy as jnp
        import numpy as np
        MODEL_DIM = 256
        FF_DIM = 1024
        NUM_EXPERTS = 8
        TOP_K = 2
        BATCH, SEQ = (4, 256)

        def _moe_forward(x, W1, b1, W2, b2, Wr, br):
            B, S, D = x.shape
            T = B * S
            xf = x.reshape(T, D)
            logits = xf @ Wr + br
            probs = jax.nn.softmax(logits, axis=-1)
            topw, topi = jax.lax.top_k(probs, TOP_K)
            topw = jax.nn.softmax(topw, axis=-1)
            comb = jnp.zeros((T, NUM_EXPERTS), dtype=xf.dtype)
            comb = comb.at[jnp.arange(T)[:, None], topi].add(topw)
            h = jax.nn.gelu(jnp.einsum('td,edf->etf', xf, W1) + b1[:, None, :], approximate=False)
            eo = jnp.einsum('etf,efd->etd', h, W2) + b2[:, None, :]
            out = jnp.einsum('etd,te->td', eo, comb)
            return out.reshape(B, S, D)
        return _moe_forward(x, W1, b1, W2, b2, Wr, br)
    x = x + _L0_xcond_ref(_layernorm(x, axis=-1), ctx_1024, ctx_1024, condB_tau[:, None], fside_BxS2_0, L0_xcond_Wq, L0_xcond_bq, L0_xcond_Wk, L0_xcond_bk, L0_xcond_Wv, L0_xcond_bv, L0_xcond_Wo, L0_xcond_bo)
    x = x + _L0_ffn_ref(_layernorm(x, axis=-1), L0_ffn_W_r, L0_ffn_W_k, L0_ffn_W_v, L0_ffn_mu_r, L0_ffn_mu_k)
    x = x + _L1_xcond_ref(_layernorm(x, axis=-1), ctx_1024, ctx_1024, condB_tau[:, None], fside_BxS2_0, L1_xcond_Wq, L1_xcond_bq, L1_xcond_Wk, L1_xcond_bk, L1_xcond_Wv, L1_xcond_bv, L1_xcond_Wo, L1_xcond_bo)
    x = x + _L1_ffn_ref(_layernorm(x, axis=-1), L1_ffn_W1, L1_ffn_b1, L1_ffn_W2, L1_ffn_b2, L1_ffn_Wr, L1_ffn_br)
    return x

_drawn_inputs = setup_inputs


def setup_inputs(seed=0):
    import zlib

    import numpy as np

    out = dict(_drawn_inputs(seed))
    spreads = {'L0_xcond_bq': (0.0, 0.329),
     'L0_xcond_bk': (0.0, 0.8),
     'L0_xcond_bv': (0.0, 0.1),
     'L0_xcond_bo': (0.0, 0.1)}
    factors = {'L0_ffn_mu_r': 4.869,
     'L1_xcond_bq': 8.0,
     'L1_xcond_bk': 8.0,
     'L1_xcond_bv': 4.711,
     'L1_xcond_bo': 4.349,
     'L1_ffn_b1': 8.0,
     'L1_ffn_b2': 5.689}
    for name, (base, spread) in spreads.items():
        noise = np.random.default_rng([zlib.crc32(name.encode()), seed]).standard_normal(out[name].shape)
        drawn = base * np.exp(spread * noise) if base else spread * noise
        out[name] = jnp.asarray(drawn.astype(out[name].dtype))
    for name, factor in factors.items():
        out[name] = (out[name] * factor).astype(out[name].dtype)
    return out
```

```python
from contextlib import ExitStack

import concourse.bass as bass
from concourse import mybir

F32, BF16 = mybir.dt.float32, mybir.dt.bfloat16
I32, U32 = mybir.dt.int32, mybir.dt.uint32
ALU = mybir.AluOpType
ACT = mybir.ActivationFunctionType
AX_X = mybir.AxisListType.X

P = 128
B, L, S, D = 4, 512, 64, 256
H, E = 16, 16
C = D // P
JT = L // P
NT = B * JT
G = H // C
PAIRS = H // 2
VW = 2 * (E + 1)
X, FF = 8, 1024
KF = FF // P
EPS = 1e-5

REGION = B * L
SLOTS = (2 * B * L - X) // P + X
SPARE = SLOTS - 2 * B * L // P
ROWS = X * REGION + SPARE * P
RW = D + 4
W1ST, W2ND, FIRST, TOKEN = range(D, RW)

PAIR = 2
TILES = PAIR * JT
ATT = PAIR * JT

WQ, WK, WV, WO = (0, 7), (1, 8), (2, 9), (3, 10)
FR, FK, FV = 4, 5, 6
MATS = 11

DELTA = 0
BO = (B * S, B * S + D)
BV = (BO[1] + D, BO[1] + 2 * D)
B1 = BV[1] + D
B2 = B1 + X * FF
BR = B2 + X * D
VECW = -(-(BR + X) // P)
VECS = VECW * P
BQ, BK, MU_R, MU_K = (0, 4), (2, 6), 8, 10
COLS = 12


def order_of_stages():
    out = []

    def norm_turned(k, g):
        out.extend(("turn", k, g, j) for j in range(JT))

    def attention(l, between):
        first, last = l * ATT, (l + 1) * ATT - 1
        out.extend([("scores", first), ("shift", first), ("exp", first)])
        for n in range(first, last + 1):
            if n < last:
                out.extend([("scores", n + 1), ("shift", n + 1)])
            out.append(("turn_probs", n))
            if n > first:
                out.append(("turn_out", n - 1))
            if n < last:
                out.append(("exp", n + 1))
            out.append(("values", n))
            if n > first:
                out.append(("project", n - 1))
            if n > first + 1:
                out.append(("norm", 2 * l + 1, (n - 2 - first) // JT, (n - 2 - first) % JT))
            out.extend(between.get(n - first, []))
        out.extend([("turn_out", last), ("project", last)])
        out.extend(("norm", 2 * l + 1, PAIR - 1, j) for j in (JT - 2, JT - 1))

    def turns(k, g):
        return [("turn", k, g, j) for j in range(JT)]

    second = {JT - 2: turns(0, 1) + [("queries", 0, 1), ("keys", 0, 1)],
              ATT - 2: turns(1, 0) + [("before", 0)], ATT - 1: [("mix", 0), ("key", 0)]}
    for j in range(JT):
        out.append(("first_stats", 0, j))
        if j:
            out.append(("norm", 0, 0, j - 1))
    out.append(("norm", 0, 0, JT - 1))
    norm_turned(0, 0)
    out.extend([("queries", 0, 0), ("keys", 0, 0)])
    for j in range(JT):
        out.append(("first_stats", 1, j))
        if j:
            out.append(("norm", 0, 1, j - 1))
    out.append(("norm", 0, 1, JT - 1))
    attention(0, second)
    out.append(("gate", 0))
    out.extend(turns(1, 1) + [("before", 1), ("mix", 1)])
    for j in range(JT):
        out.append(("value", 0, j))
        if j:
            out.append(("norm", 2, 0, j - 1))
    out.append(("norm", 2, 0, JT - 1))
    out.extend([("key", 1), ("gate", 1)])
    out.extend(turns(2, 0))
    for j in range(JT):
        out.append(("value", 1, j))
        if j:
            out.append(("norm", 2, 1, j - 1))
    out.append(("norm", 2, 1, JT - 1))
    out.extend([("keys", 1, 0), ("queries", 1, 0)])
    second = {JT - 2: turns(2, 1) + [("keys", 1, 1), ("queries", 1, 1)], ATT - 2: turns(3, 0)}
    attention(1, second)
    out.extend(turns(3, 1))
    out.extend([("logits",), ("choose",), ("ranks",), ("places",), ("scatter",)])
    return out


ORDER = order_of_stages()
TURN = {s: n for n, s in enumerate(x for x in ORDER if x[0] in ("turn", "turn_out", "logits", "ranks"))}
ADDED = {s: n for n, s in enumerate(x for x in ORDER if x[0] in ("project", "value"))}


class Signal:

    def __init__(self, sem, per):
        self.sem, self.per = sem, per

    def value(self, i, k):
        return i * self.per + k


def build(nc, x_in, ctx_in, tau_in, mats_in, cols_in, vecs_in, w1_in, w2_in, wr_in, out):
    routed = nc.dram_tensor("routed_rows", (ROWS, RW), F32, kind="Internal").ap()
    stack = ExitStack()
    with stack:
        def sb(name, shape, dt=F32):
            return stack.enter_context(nc.sbuf_tensor(name, shape, dt))

        def pb(name, width):
            return stack.enter_context(nc.psum_tensor(name, [P, width], F32))

        def sem(name):
            return stack.enter_context(nc.semaphore(name))

        def signal(name, per):
            return Signal(sem(name), per)

        EW = C * FF + KF * D
        EARLY = 4
        experts = sb("experts", [P, X * EW])
        room = [EARLY * EW]

        def lent(*dims):
            n = 1
            for d in dims:
                n *= d
            a = experts[:, room[0]:room[0] + n]
            room[0] += n
            assert room[0] <= X * EW
            names = "abcd"[:len(dims)]
            if len(dims) > 1:
                kw = {names[i]: dims[i] for i in range(1, len(dims))}
                a = a.rearrange(f"p ({' '.join(names)}) -> p {' '.join(names)}", **kw)
            return a

        vbd = lent(2 * B * PAIRS, VW)
        keys = lent(2 * C, B * S)
        mats = lent(MATS * C, D)
        kbd = lent(PAIR, C, G * S)
        shifted = lent(L * C)
        assert room[0] <= (X - 1) * EW
        qT = lent(PAIR, C, L)
        xnT = lent(PAIR, C, L + 1)

        def mat(m, c):
            return mats[:, m * C + c, :]

        x = sb("x", [P, NT, D])
        rows3 = sb("rows3", [P, VECS], BF16)
        xn = sb("xn", [P, TILES, RW])
        probs = sb("probs", [P, H * S])
        probsT = sb("probsT", [P, PAIRS, P])
        onorm = sb("onorm", [P, D])
        oT = sb("oT", [P, 2, C, P])
        gated = oT[:, 0, :, :].rearrange("p c t -> p (c t)")
        ident = sb("ident", [P, P])
        tri = sb("tri", [P, P], BF16)
        ones = sb("ones", [P, P], BF16)
        quarter = sb("quarter", [P, P], BF16)
        mask = sb("mask", [P, G])
        cols = sb("cols", [P, COLS])
        omu = sb("omu", [P, 4])
        wr = sb("wr", [P, C, X])
        tau = sb("tau", [P, B])
        halfneg = sb("halfneg", [P, 1])
        fstat = sb("fstat", [P, TILES, 6])
        mv = sb("mv", [P, TILES, 2])
        veps = sb("veps", [P, TILES])
        rstd = sb("rstd", [P, TILES])
        smax = sb("smax", [P, H])
        rsum = sb("rsum", [P, H])
        r8 = sb("r8", [P, 11, TILES, X])
        r1 = sb("r1", [P, 10, TILES])
        ranks = sb("ranks", [P, 2, TILES, X])
        chosen = sb("chosen", [P, TILES, X], BF16)
        iota8 = sb("iota8", [P, X])
        iota8m = sb("iota8m", [P, X])
        region = sb("region", [P, X])
        token = sb("token", [P, NT])
        count = sb("count", [P, X])
        where_ = sb("where", [P, 2, TILES], U32)
        vecs = sb("vecs", [P, VECW])
        vres = sb("vres", [P, 2, VECW])
        vpart = sb("vpart", [P, 3, VECW], BF16)
        ctxT = probs[:, :].rearrange("p (c b s) -> p c b s", c=C, b=B)

        xg = xn[:, 0, :]
        xgT = oT[:, 0, :, :]
        hid = probs
        hidT = probsT
        ysb = onorm
        empty = sb("empty", [P, RW])
        slot_cols = sb("slot_cols", [P, SLOTS, RW - D])
        slot_w = sb("slot_w", [P, SLOTS, 3])
        slot_tok = sb("slot_tok", [P, 1], U32)
        iota_s = sb("iota_s", [P, SLOTS])
        ge = probs[:, 0:SLOTS * X].rearrange("p (s e) -> p s e", e=X)
        gen = probs[:, SLOTS * X:2 * SLOTS * X].rearrange("p (s e) -> p s e", e=X)
        tt = sb("tt", [P, 4, X])
        tti = sb("tti", [P, X], I32)
        st = sb("st", [P, 5, SLOTS])
        slot_row = sb("slot_row", [1, SLOTS], I32)
        slot_exp = sb("slot_exp", [1, SLOTS], I32)

        ps_t = [pb("ps_t0", 512), pb("ps_t1", 512)]
        ps_s = pb("ps_s", 1024)
        ps_p = pb("ps_p", 1024)
        ps_o = pb("ps_o", 512)
        ps_w = pb("ps_w", 512)

        ld_ctx, ld_mats, ld_small, ld_x, ld_vecs = (sem(n) for n in ("ld_ctx", "ld_mats", "ld_small", "ld_x", "ld_vecs"))
        ld_rows3, ld_fill, ld_early, ld_late = (sem(n) for n in ("ld_rows3", "ld_fill", "ld_early", "ld_late"))
        const_ready = sem("const_ready")
        const_step = sem("const_step")
        split_ready = sem("split_ready")
        pre_step = sem("pre_step")
        pre_mm = sem("pre_mm")
        pre_ev = sem("pre_ev")

        DVE_STEPS = 116
        dve_step = signal("dve_step", DVE_STEPS)
        pool_step = signal("pool_step", 32)
        mv_ready = signal("mv_ready", 32)
        rstd_ready = signal("rstd_ready", 32)
        xn_ready = signal("xn_ready", 32)
        turned = signal("turned", len(TURN))
        turn_read = signal("turn_read", len(TURN))
        q_done = signal("q_done", 2 * PAIR * C)
        q_out = signal("q_out", 2 * PAIR * C)
        kbd_ready = signal("kbd_ready", 2 * PAIR * C)
        s_done = signal("s_done", 2 * ATT)
        sub_done = signal("sub_done", 2 * ATT)
        exp_done = signal("exp_done", 2 * ATT)
        pt_done = signal("pt_done", 2 * ATT)
        pt_out = signal("pt_out", 2 * ATT)
        pv_done = signal("pv_done", 2 * ATT)
        on_done = signal("on_done", 2 * ATT)
        pr_done = signal("pr_done", 2 * ATT)
        x_done = signal("x_done", len(ADDED))
        prev_done = signal("prev_done", PAIR * 2 * C)
        mix_done = signal("mix_done", PAIR * 2 * C)
        key_done = signal("key_done", PAIR * C)
        relu_done = signal("relu_done", PAIR * C)
        kact_done = signal("kact_done", PAIR * C)
        rg_done = signal("rg_done", PAIR * 2)
        gate_done = signal("gate_done", PAIR * 2)
        val_done = signal("val_done", PAIR * JT)
        lsub_done = signal("lsub_done", 1)
        lexp_done = signal("lexp_done", 1)
        gap_done = signal("gap_done", 1)
        gexp_done = signal("gexp_done", 1)
        chosen_done = signal("chosen_done", 1)
        packed_done = signal("packed_done", 1)
        scattered = signal("scattered", 16 * 2 * TILES)
        passed = sem("passed")
        xout = sem("xout")

        tab_step = sem("tab_step")
        tables = sem("tables")
        xg_loaded = sem("xg_loaded")
        wi_out = sem("wi_out")
        xt_done = sem("xt_done")
        xt_out = sem("xt_out")
        hid_done = sem("hid_done")
        gelu_done = sem("gelu_done")
        ht_done = sem("ht_done")
        ht_out = sem("ht_out")
        y_done = sem("y_done")
        ps_y_free = sem("ps_y_free")
        tok_out = sem("tok_out")
        ysb_free = sem("ysb_free")
        added = sem("added")

        PRE_KEYS = 2 * C * B
        PRE_VALS = 2 * B * 2

        def mixed(w, g, c):
            return (qT, kbd)[w][:, g, c, :]

        def kact(g, c):
            return xnT[:, g, c, 1:L + 1]

        def gate_of(g, half):
            return qT[:, g, half, :]

        def stage_of(own):
            for stage, *which in ORDER:
                if stage in own:
                    own[stage](*which)

        def load_expert(eng, e, done):
            at = e * EW
            eng.dma_start(experts[:, at:at + C * FF].rearrange("p (c f) -> p c f", c=C),
                          w1_in[e].rearrange("(c p) f -> p c f", p=P)).then_inc(done, 16)
            eng.dma_start(experts[:, at + C * FF:at + EW].rearrange("p (k d) -> p k d", k=KF),
                          w2_in[e].rearrange("(k p) d -> p k d", p=P)).then_inc(done, 16)

        block = stack.enter_context(nc.Block())

        @block.sync
        def _(sp):
            sp.dma_start(ctxT, ctx_in.rearrange("(c p) (b s) -> p c b s", p=P, b=B)).then_inc(ld_ctx, 16)
            src = mats_in.rearrange("m (c p) n -> p (m c) n", p=P)
            sp.dma_start(mats, src).then_inc(ld_mats, 16)
            sp.dma_start(x[:, :, :], x_in.rearrange("(t p) d -> p t d", p=P)).then_inc(ld_x, 16)
            sp.wait_ge(split_ready, 4)
            for i in range(3):
                sp.dma_start(rows3[i:i + 1, :].rearrange("o (p k) -> o p k", k=VECW), vpart[:, i, :]).then_inc(ld_rows3, 16)
            sp.wait_ge(const_ready, 1)
            sp.dma_start(routed.rearrange("(n p) k -> p n k", p=P),
                         empty[:, :].unsqueeze(1).to_broadcast([P, ROWS // P, RW])).then_inc(ld_fill, 16)
            for e in range(EARLY):
                load_expert(sp, e, ld_early)
            with sp.Fori(0, B // PAIR) as i:
                sp.wait_ge(x_done.sem, x_done.value(i, x_done.per))
                sp.dma_start(out[0:B * L, :].rearrange("(t p) d -> p t d", p=P)[:, bass.ds(i * TILES, TILES), :],
                             x[:, bass.ds(i * TILES, TILES), :]).then_inc(xout, 16)
            for e in range(EARLY, X - 1):
                load_expert(sp, e, ld_late)
            sp.wait_ge(packed_done.sem, B // PAIR)
            load_expert(sp, X - 1, ld_late)
            sp.wait_ge(tables, 2)
            sp.wait_ge(scattered.sem, B // PAIR * scattered.per)

            def load_slot(s):
                row = sp.value_load(slot_row[0:1, bass.ds(s, 1)], min_val=0, max_val=ROWS - P)
                sp.dma_start(xg, routed[bass.ds(row, P), :]).then_inc(xg_loaded, 16)

            load_slot(0)
            with sp.Fori(1, SLOTS) as s:
                sp.wait_ge(xt_done, s)
                sp.wait_ge(wi_out, s)
                load_slot(s)

        @block.gpsimd
        def _(pool):
            fill = empty[:, :]
            pool.memset(fill, 0.0).then_inc(const_step, 1)
            pool.wait_ge(const_step, 1)
            pool.iota(fill[:, TOKEN:TOKEN + 1], [[0, 1]], base=B * L, channel_multiplier=1,
                      allow_small_or_imprecise_dtypes=True).then_inc(const_ready, 1)
            pool.memset(ident[:, :], 0.0).then_inc(const_step, 1)
            pool.memset(tri[:, :], 1.0).then_inc(const_step, 1)
            pool.memset(mask[:, :], 1.0).then_inc(const_step, 1)
            pool.memset(ones[:, :], 1.0).then_inc(const_ready, 1)
            pool.memset(quarter[:, :], 0.25).then_inc(const_ready, 1)
            pool.memset(halfneg[:, :], -0.5).then_inc(const_step, 1)
            pool.memset(xnT[:, :, :, 0:1], 0.0).then_inc(const_ready, 1)
            pool.wait_ge(const_step, 5)
            pool.affine_select(out=ident[:, :], in_=ident[:, :], compare_op=ALU.not_equal, fill=1.0, base=0,
                               pattern=[[-1, P]], channel_multiplier=1).then_inc(const_ready, 1)
            pool.affine_select(out=tri[:, :], in_=tri[:, :], compare_op=ALU.is_gt, fill=0.0, base=0,
                               pattern=[[1, P]], channel_multiplier=-1).then_inc(const_ready, 1)
            pool.affine_select(out=mask[:, :], in_=mask[:, :], compare_op=ALU.is_ge, fill=0.0, base=0,
                               pattern=[[-E, G]], channel_multiplier=1).then_inc(const_step, 1)
            pool.wait_ge(const_step, 6)
            pool.affine_select(out=mask[:, :], in_=mask[:, :], compare_op=ALU.is_ge, fill=0.0, base=E - 1,
                               pattern=[[E, G]], channel_multiplier=-1).then_inc(const_step, 1)
            pool.iota(iota8[:, :], [[1, X]], base=0, channel_multiplier=0, allow_small_or_imprecise_dtypes=True).then_inc(const_ready, 1)
            pool.iota(iota8m[:, :], [[1, X]], base=-X, channel_multiplier=0, allow_small_or_imprecise_dtypes=True).then_inc(const_ready, 1)
            pool.iota(region[:, :], [[REGION, X]], base=0, channel_multiplier=0, allow_small_or_imprecise_dtypes=True).then_inc(const_ready, 1)
            pool.iota(iota_s[:, :], [[1, SLOTS]], base=0, channel_multiplier=0, allow_small_or_imprecise_dtypes=True).then_inc(const_ready, 1)
            pool.iota(token[:, :], [[P, NT]], base=0, channel_multiplier=1, allow_small_or_imprecise_dtypes=True).then_inc(const_ready, 1)
            pool.wait_ge(const_step, 7)

            pool.wait_ge(pre_ev, PRE_KEYS)
            with pool.Fori(0, B // PAIR) as i:
                def norm(k, g, j):
                    t = g * JT + j
                    n = k * TILES + t + 1
                    pool.wait_ge(mv_ready.sem, mv_ready.value(i, n))
                    pool.sem_inc(passed, 1)
                    pool.tensor_scalar(veps[:, t:t + 1], mv[:, t, 1:2], EPS, None, ALU.add).then_inc(pool_step.sem, 1)
                    pool.wait_ge(pool_step.sem, pool_step.value(i, n))
                    pool.tensor_tensor(rstd[:, t:t + 1], veps[:, t:t + 1], halfneg[:, :], ALU.pow).then_inc(rstd_ready.sem, 1)

                def block_diagonal_keys(l, g):
                    if l == 1:
                        pool.wait_ge(rg_done.sem, rg_done.value(i, 2 * (g + 1)))
                    for c in range(C):
                        pool.tensor_tensor(
                            kbd[:, g, c, :].rearrange("p (h s) -> p h s", h=G),
                            keys[:, l * C + c, bass.ds((i * PAIR + g) * S, S)].unsqueeze(1).to_broadcast([P, G, S]),
                            mask[:, :].unsqueeze(2).to_broadcast([P, G, S]), ALU.mult).then_inc(kbd_ready.sem, 1)

                def scatter():
                    pool.wait_ge(packed_done.sem, packed_done.value(i, 1))
                    pool.sem_inc(passed, 1)
                    pool.wait_ge(ld_fill, 16)
                    for k in range(2):
                        for t in range(TILES):
                            pool.indirect_dma_start(
                                out=routed, out_offset=bass.IndirectOffsetOnAxis(ap=where_[:, k, t:t + 1], axis=0),
                                in_=xn[:, t, :], in_offset=None).then_inc(scattered.sem, 16)
                    pool.wait_ge(scattered.sem, scattered.value(i, scattered.per))

                stage_of({"norm": norm, "keys": block_diagonal_keys, "scatter": scatter})

            pool.wait_ge(xout, 16 * (B // PAIR + 1))

            with pool.Fori(0, SLOTS) as s:
                pool.wait_ge(tok_out, s + 1)
                pool.sem_inc(passed, 1)
                pool.indirect_dma_start(out=out, out_offset=bass.IndirectOffsetOnAxis(ap=slot_tok[:, 0:1], axis=0),
                                        in_=ysb[:, :], in_offset=None, compute_op=ALU.add).then_inc(added, 16)
                pool.wait_ge(added, 16 * s + 16)
                pool.sem_inc(ysb_free, 1)

        @block.scalar
        def _(act):
            act.dma_start(vecs[:, :], vecs_in.rearrange("(p k) -> p k", k=VECW)).then_inc(ld_vecs, 16)
            act.dma_start(cols[:, :], cols_in).then_inc(ld_small, 16)
            act.dma_start(tau[:, :], tau_in.rearrange("(o b) -> o b", o=1).partition_broadcast(P).rearrange("p o b -> p (o b)")).then_inc(ld_small, 16)
            act.dma_start(wr[:, :, :], wr_in.rearrange("(c p) e -> p c e", p=P)).then_inc(ld_small, 16)
            act.wait_ge(const_ready, 1)
            act.dma_start(out[B * L:B * L + P, :], empty[:, 0:D]).then_inc(xout, 16)

            act.wait_ge(ld_small, 48)
            act.wait_ge(pre_step, 1)
            with act.Fori(0, B // PAIR) as i:
                def copy_turned(n, to, width):
                    act.wait_ge(turned.sem, turned.value(i, n + 1))
                    act.activation(to, ps_t[n % 2][:, 0:width], ACT.Copy).then_inc(turn_read.sem, 1)

                def turn(k, g, j):
                    copy_turned(TURN["turn", k, g, j], xnT[:, g, :, 1 + j * P:1 + (j + 1) * P], D)

                def turn_out(n):
                    copy_turned(TURN["turn_out", n], oT[:, n % 2, :, :], D)

                def queries(l, g):
                    for c in range(C):
                        n = (PAIR * l + g) * C + c + 1
                        act.wait_ge(q_done.sem, q_done.value(i, n))
                        act.activation(qT[:, g, c, :], (ps_w, ps_o)[c][:, :], ACT.Identity,
                                       bias=cols[:, BQ[l] + c:BQ[l] + c + 1]).then_inc(q_out.sem, 1)

                def exp(n):
                    act.wait_ge(sub_done.sem, sub_done.value(i, n + 1))
                    if n:
                        act.wait_ge(pt_done.sem, pt_done.value(i, n))
                    act.activation(probs[:, :], shifted, ACT.Exp).then_inc(exp_done.sem, 1)

                def turn_probs(n):
                    act.wait_ge(pt_done.sem, pt_done.value(i, n + 1))
                    if n:
                        act.wait_ge(pv_done.sem, pv_done.value(i, n))
                    act.activation(probsT[:, :, :].rearrange("p a t -> p (a t)"), ps_p[:, :], ACT.Copy).then_inc(pt_out.sem, 1)

                def before(g):
                    act.wait_ge(turn_read.sem, turn_read.value(i, TURN["turn", 1, g, JT - 1] + 1))
                    for w in range(2):
                        for c in range(C):
                            act.activation(mixed(w, g, c), xnT[:, g, c, 0:L], ACT.Copy,
                                           scale=omu[:, 2 * (1 - w) + c:2 * (1 - w) + c + 1]).then_inc(prev_done.sem, 1)

                def key(g):
                    for c in range(C):
                        act.wait_ge(key_done.sem, key_done.value(i, g * C + c + 1))
                        if c == 0:
                            act.wait_ge(mix_done.sem, mix_done.value(i, (g + 1) * 2 * C))
                        act.activation(kact(g, c), ps_s[:, c * L:(c + 1) * L], ACT.Relu).then_inc(relu_done.sem, 1)

                def gate(g):
                    for half in range(2):
                        act.wait_ge(rg_done.sem, rg_done.value(i, g * 2 + half + 1))
                        act.activation(gate_of(g, half), ps_p[:, half * 512:(half + 1) * 512], ACT.Tanh,
                                       scale=0.5).then_inc(gate_done.sem, 1)

                def logits():
                    copy_turned(TURN["logits",], r8[:, 10].rearrange("p t e -> p (t e)"), TILES * X)

                def choose():
                    act.wait_ge(lsub_done.sem, lsub_done.value(i, 1))
                    act.activation(r8[:, 1], r8[:, 0], ACT.Exp).then_inc(lexp_done.sem, 1)
                    act.wait_ge(gap_done.sem, gap_done.value(i, 1))
                    act.activation(r1[:, 7], r1[:, 6], ACT.Exp).then_inc(gexp_done.sem, 1)

                def ranked():
                    copy_turned(TURN["ranks",], ranks[:, :, :, :].rearrange("p a t e -> p (a t e)"), 2 * TILES * X)

                stage_of({"turn": turn, "turn_out": turn_out, "queries": queries, "exp": exp, "turn_probs": turn_probs,
                          "before": before, "key": key, "gate": gate, "logits": logits, "choose": choose,
                          "ranks": ranked})

            def xgT_out(n_done):
                act.wait_ge(xt_done, n_done)
                act.activation(xgT, ps_t[0][:, 0:D].rearrange("p (c t) -> p c t", c=C), ACT.Copy).then_inc(xt_out, 1)

            def gelu(s, half):
                act.wait_ge(hid_done, 2 * s + half + 1)
                act.activation(hid[:, half * 512:(half + 1) * 512], ps_s[:, half * 512:(half + 1) * 512],
                               ACT.Gelu).then_inc(gelu_done, 1)

            xgT_out(1)
            gelu(0, 0)
            gelu(0, 1)
            xgT_out(2)
            with act.Fori(0, SLOTS - 2) as s:
                act.wait_ge(hid_done, 2 * s + 3)
                act.wait_ge(ht_done, s + 1)
                gelu(s + 1, 0)
                gelu(s + 1, 1)
                xgT_out(s + 3)
            act.wait_ge(ht_done, SLOTS - 1)
            gelu(SLOTS - 1, 0)
            gelu(SLOTS - 1, 1)

        @block.tensor
        def _(pe):
            pe.wait_ge(ld_ctx, 16)
            pe.wait_ge(ld_mats, 16)
            n = 0
            for l in range(2):
                for c in range(C):
                    bank = (ps_w, ps_o)[n % 2]
                    if n >= 2:
                        pe.wait_ge(pre_ev, B * (n - 1))
                    for k in range(C):
                        mm = pe.matmul(bank[:, 0:B * S], mat(WK[l], k)[:, c * P:(c + 1) * P], ctxT[:, k, :, 0:S],
                                       start=(k == 0), stop=(k == C - 1))
                    mm.then_inc(pre_mm, 1)
                    n += 1
            pe.wait_ge(const_ready, 5)
            pe.wait_ge(ld_rows3, 48)
            m = 0
            for l in range(2):
                for b in range(B):
                    bank = (ps_w, ps_o)[m % 2]
                    pe.wait_ge(pre_ev, PRE_KEYS - B + B * m if m < 2 else PRE_KEYS + 2 * (m - 1))
                    for k in range(C):
                        pe.matmul(bank[:, 0:D], ctxT[:, k, b, :], mat(WV[l], k), start=(k == 0), stop=False)
                    pe.matmul(bank[:, 0:D], ones[:, :], rows3[:, BV[l]:BV[l] + D], start=False, stop=True).then_inc(pre_mm, 1)
                    m += 1
            pe.wait_ge(pre_ev, PRE_KEYS + PRE_VALS)
            with pe.Fori(0, B // PAIR) as i:
                frees = {}

                def wait_free(bank):
                    if bank in frees:
                        signal_, n = frees[bank]
                        pe.wait_ge(signal_.sem, signal_.value(i, n))

                def turn_bank(n):
                    if n >= 2:
                        pe.wait_ge(turn_read.sem, turn_read.value(i, n - 1))
                    return ps_t[n % 2]

                def transposed(n, tile):
                    bank = turn_bank(n)
                    for c in range(C):
                        mm = pe.transpose(bank[:, c * P:(c + 1) * P], tile[:, c * P:(c + 1) * P], ident[:, :])
                    mm.then_inc(turned.sem, 1)

                def turn(k, g, j):
                    pe.wait_ge(xn_ready.sem, xn_ready.value(i, k * TILES + g * JT + j + 1))
                    transposed(TURN["turn", k, g, j], xn[:, g * JT + j, 0:D])

                def queries(l, g):
                    pe.wait_ge(turn_read.sem, turn_read.value(i, TURN["turn", 2 * l, g, JT - 1] + 1))
                    for c in range(C):
                        n = (PAIR * l + g) * C + c + 1
                        wait_free("wo"[c])
                        for k in range(C):
                            mm = pe.matmul((ps_w, ps_o)[c][:, :], mat(WQ[l], k)[:, c * P:(c + 1) * P],
                                           xnT[:, g, k, 1:L + 1], start=(k == 0), stop=(k == C - 1))
                        mm.then_inc(q_done.sem, 1)
                        frees["wo"[c]] = (q_out, n)

                def scores(n):
                    l, g, j = n // ATT, n % ATT // JT, n % JT
                    if j == 0:
                        pe.wait_ge(q_out.sem, q_out.value(i, (PAIR * l + g + 1) * C))
                        pe.wait_ge(kbd_ready.sem, kbd_ready.value(i, (PAIR * l + g + 1) * C))
                    if n:
                        pe.wait_ge(sub_done.sem, sub_done.value(i, n))
                    if n == ATT:
                        pe.wait_ge(relu_done.sem, relu_done.value(i, PAIR * C))
                    for c in range(C):
                        pe.matmul(ps_s[:, c * 512:(c + 1) * 512], qT[:, g, c, j * P:(j + 1) * P], kbd[:, g, c, :],
                                  start=True, stop=False)
                        mm = pe.matmul(ps_s[:, c * 512:(c + 1) * 512].rearrange("p (h s) -> p h s", h=G), quarter[:, :],
                                       rows3[:, bass.ds((i * PAIR + g) * S + DELTA, S)].unsqueeze(1).to_broadcast([P, G, S]),
                                       start=False, stop=True)
                    mm.then_inc(s_done.sem, 1)

                def turn_probs(n):
                    pe.wait_ge(exp_done.sem, exp_done.value(i, n + 1))
                    if n == ATT:
                        pe.wait_ge(gate_done.sem, gate_done.value(i, PAIR * 2))
                    for a in range(PAIRS):
                        mm = pe.transpose(ps_p[:, a * P:(a + 1) * P], probs[:, a * P:(a + 1) * P], ident[:, :])
                    mm.then_inc(pt_done.sem, 1)

                def values(n):
                    l, g = n // ATT, n % ATT // JT
                    pe.wait_ge(pt_out.sem, pt_out.value(i, n + 1))
                    wait_free("o")
                    for a in range(PAIRS):
                        mm = pe.matmul(ps_o[:, a * VW:(a + 1) * VW], probsT[:, a, :],
                                       vbd[:, bass.ds((i * PAIR + g) * PAIRS + (l * B * PAIRS + a), 1), :].rearrange("p a w -> p (a w)"),
                                       start=True, stop=True)
                    mm.then_inc(pv_done.sem, 1)
                    frees["o"] = (on_done, n + 1)

                def turn_out(n):
                    pe.wait_ge(on_done.sem, on_done.value(i, n + 1))
                    transposed(TURN["turn_out", n], onorm[:, :])

                def project(n):
                    l = n // ATT
                    pe.wait_ge(turn_read.sem, turn_read.value(i, TURN["turn_out", n] + 1))
                    wait_free("w")
                    for k in range(C):
                        pe.matmul(ps_w[:, 0:D], oT[:, n % 2, k, :], mat(WO[l], k), start=(k == 0), stop=False)
                    pe.matmul(ps_w[:, 0:D], ones[:, :], rows3[:, BO[l]:BO[l] + D], start=False, stop=True).then_inc(pr_done.sem, 1)
                    frees["w"] = (x_done, ADDED["project", n] + 1)

                def key(g):
                    pe.wait_ge(mix_done.sem, mix_done.value(i, g * 2 * C + C))
                    if g == 0:
                        pe.wait_ge(sub_done.sem, sub_done.value(i, ATT))
                    else:
                        pe.wait_ge(relu_done.sem, relu_done.value(i, g * C))
                    for c in range(C):
                        for k in range(C):
                            mm = pe.matmul(ps_s[:, c * L:(c + 1) * L], mat(FK, k)[:, c * P:(c + 1) * P], mixed(0, g, k),
                                           start=(k == 0), stop=(k == C - 1))
                        mm.then_inc(key_done.sem, 1)

                def gate(g):
                    pe.wait_ge(mix_done.sem, mix_done.value(i, (g + 1) * 2 * C))
                    if g == 0:
                        pe.wait_ge(pt_out.sem, pt_out.value(i, ATT))
                    else:
                        pe.wait_ge(gate_done.sem, gate_done.value(i, g * 2))
                    for j in range(JT):
                        for k in range(C):
                            mm = pe.matmul(ps_p[:, j * D:(j + 1) * D], mixed(1, g, k)[:, j * P:(j + 1) * P], mat(FR, k),
                                           start=(k == 0), stop=(k == C - 1))
                        if j % 2:
                            mm.then_inc(rg_done.sem, 1)

                def value(g, j):
                    if j == 0:
                        pe.wait_ge(kact_done.sem, kact_done.value(i, (g + 1) * C))
                    wait_free("wo"[j % 2])
                    for k in range(C):
                        mm = pe.matmul((ps_w, ps_o)[j % 2][:, 0:D], kact(g, k)[:, j * P:(j + 1) * P], mat(FV, k),
                                       start=(k == 0), stop=(k == C - 1))
                    mm.then_inc(val_done.sem, 1)
                    frees["wo"[j % 2]] = (x_done, ADDED["value", g, j] + 1)

                def logits():
                    n = TURN["logits",]
                    bank = turn_bank(n)
                    pe.wait_ge(turn_read.sem, turn_read.value(i, n))
                    for t in range(TILES):
                        to = bank[:, t * X:(t + 1) * X]
                        for k in range(C):
                            pe.matmul(to, xnT[:, t // JT, k, 1 + t % JT * P:1 + (t % JT + 1) * P], wr[:, k, :],
                                      start=(k == 0), stop=False)
                        mm = pe.matmul(to, ones[:, :], rows3[:, BR:BR + X], start=False, stop=True)
                    mm.then_inc(turned.sem, 1)

                def ranked():
                    bank = turn_bank(TURN["ranks",])
                    pe.wait_ge(chosen_done.sem, chosen_done.value(i, 1))
                    picks = chosen[:, :, :].rearrange("p t e -> p (t e)")
                    pe.matmul(bank[:, 0:TILES * X], tri[:, :], picks, start=True, stop=True)
                    pe.matmul(bank[:, TILES * X:2 * TILES * X], ones[:, :], picks, start=True, stop=True).then_inc(turned.sem, 1)

                stage_of({"turn": turn, "queries": queries, "scores": scores, "turn_probs": turn_probs, "values": values,
                          "turn_out": turn_out, "project": project, "key": key, "gate": gate, "value": value,
                          "logits": logits, "ranks": ranked})

            def expert_of(s):
                return pe.value_load(slot_exp[0:1, bass.ds(s, 1)], min_val=0, max_val=X - 1)

            def rows_transposed(n_loaded):
                pe.wait_ge(xg_loaded, n_loaded)
                for c in range(C):
                    mm = pe.transpose(ps_t[0][:, c * P:(c + 1) * P], xg[:, c * P:(c + 1) * P], ident[:, :])
                mm.then_inc(xt_done, 1)

            def hidden(e, half):
                to = ps_s[:, half * 512:(half + 1) * 512]
                pe.matmul(to, ones[:, :], rows3[:, bass.ds(e * FF + (B1 + half * 512), 512)], start=True, stop=False)
                for c in range(C):
                    mm = pe.matmul(to, xgT[:, c, :], experts[:, bass.ds(e * EW + (c * FF + half * 512), 512)],
                                   start=False, stop=(c == C - 1))
                mm.then_inc(hid_done, 1)

            def hidden_transposed():
                for k in range(KF):
                    mm = pe.transpose(ps_p[:, k * P:(k + 1) * P], hid[:, k * P:(k + 1) * P], ident[:, :])
                mm.then_inc(ht_done, 1)

            def result(e):
                pe.matmul(ps_w[:, 0:D], ones[:, :], rows3[:, bass.ds(e * D + B2, D)], start=True, stop=False)
                for k in range(KF):
                    mm = pe.matmul(ps_w[:, 0:D], hidT[:, k, :], experts[:, bass.ds(e * EW + (C * FF + k * D), D)],
                                   start=False, stop=(k == KF - 1))
                mm.then_inc(y_done, 1)

            pe.wait_ge(tables, 2)
            rows_transposed(16)
            pe.wait_ge(ld_early, 32 * EARLY)
            pe.wait_ge(ld_late, 32 * (X - EARLY))
            pe.wait_ge(xt_out, 1)
            first = expert_of(0)
            hidden(first, 0)
            hidden(first, 1)
            rows_transposed(32)
            with pe.Fori(0, SLOTS - 2) as s:
                nxt = expert_of(s + 1)
                pe.wait_ge(gelu_done, 2 * s + 1)
                pe.wait_ge(xt_out, s + 2)
                hidden(nxt, 0)
                pe.wait_ge(gelu_done, 2 * s + 2)
                hidden_transposed()
                hidden(nxt, 1)
                own = expert_of(s)
                rows_transposed(16 * s + 48)
                pe.wait_ge(ht_out, 2 * s + 2)
                pe.wait_ge(ps_y_free, s + 1)
                result(own)
            nxt = expert_of(SLOTS - 1)
            pe.wait_ge(gelu_done, 2 * SLOTS - 3)
            pe.wait_ge(xt_out, SLOTS)
            hidden(nxt, 0)
            pe.wait_ge(gelu_done, 2 * SLOTS - 2)
            hidden_transposed()
            hidden(nxt, 1)
            own = expert_of(SLOTS - 2)
            pe.wait_ge(ht_out, 2 * SLOTS - 2)
            pe.wait_ge(ps_y_free, SLOTS - 1)
            result(own)
            pe.wait_ge(gelu_done, 2 * SLOTS)
            hidden_transposed()
            own = expert_of(SLOTS - 1)
            pe.wait_ge(ht_out, 2 * SLOTS)
            pe.wait_ge(ps_y_free, SLOTS)
            result(own)

        @block.vector
        def _(dve):
            dve.memset(rows3[:, :].bitcast(F32), 0.0).then_inc(split_ready, 1)
            dve.wait_ge(ld_vecs, 16)
            done = [0]

            def step(ins):
                done[0] += 1
                ins.then_inc(pre_step, 1)
                dve.wait_ge(pre_step, done[0])

            dve.wait_ge(ld_small, 48)
            step(dve.tensor_scalar(omu[:, :], cols[:, MU_R:MU_R + 4], -1.0, 1.0, ALU.mult, ALU.add))
            step(dve.tensor_scalar(tau[:, :], tau[:, :], 1.0 / E ** 0.5, None, ALU.mult))
            dve.tensor_copy(vpart[:, 0, :], vecs[:, :]).then_inc(split_ready, 1)
            dve.wait_ge(split_ready, 2)
            step(dve.tensor_tensor(vres[:, 0, :], vecs[:, :], vpart[:, 0, :], ALU.subtract))
            dve.tensor_copy(vpart[:, 1, :], vres[:, 0, :]).then_inc(split_ready, 1)
            dve.wait_ge(split_ready, 3)
            step(dve.tensor_tensor(vres[:, 1, :], vres[:, 0, :], vpart[:, 1, :], ALU.subtract))
            dve.tensor_copy(vpart[:, 2, :], vres[:, 1, :]).then_inc(split_ready, 1)
            dve.memset(vbd[:, :, :], 0.0).then_inc(pre_step, 1)
            dve.memset(count[:, :], 0.0).then_inc(pre_step, 1)
            done[0] += 2
            dve.wait_ge(pre_step, done[0])
            n = 0
            for l in range(2):
                for c in range(C):
                    dve.wait_ge(pre_mm, n + 1)
                    for b in range(B):
                        dve.tensor_scalar(keys[:, l * C + c, b * S:(b + 1) * S], (ps_w, ps_o)[n % 2][:, b * S:(b + 1) * S],
                                          cols[:, BK[l] + c:BK[l] + c + 1], tau[:, b:b + 1], ALU.add, ALU.mult).then_inc(pre_ev, 1)
                    n += 1
            for l in range(2):
                for b in range(B):
                    dve.wait_ge(pre_mm, n + 1)
                    for q in range(2):
                        half = slice(q * S, (q + 1) * S)
                        at = (l * B + b) * PAIRS
                        to = vbd[half, at:at + PAIRS, q * (E + 1):q * (E + 1) + E]
                        frm = (ps_w, ps_o)[n % 2][half, 0:D].rearrange("s (a q d) -> s a q d", q=2, d=E)[:, :, q, :]
                        dve.tensor_copy(to, frm).then_inc(pre_ev, 1)
                    n += 1
            for q in range(2):
                col = q * (E + 1) + E
                step(dve.memset(vbd[q * S:(q + 1) * S, :, col:col + 1], 1.0))
            dve.wait_ge(const_ready, 11)
            dve.wait_ge(ld_x, 16)

            links = [0]

            def mark(ins):
                links[0] += 1
                ins.then_inc(dve_step.sem, 1)
                return links[0]

            def link(b, ins):
                n = mark(ins)
                dve.wait_ge(dve_step.sem, dve_step.value(b, n))

            with dve.Fori(0, B // PAIR) as i:
                links[0] = 0

                def tile_of(t):
                    return x[:, bass.ds(i * TILES + t, 1), :].rearrange("p t d -> p (t d)")

                def statistics(t):
                    dve.sem_inc(passed, 1)
                    link(i, dve.bn_stats(fstat[:, t, :], tile_of(t)))
                    dve.sem_inc(passed, 1)
                    dve.bn_aggr(mv[:, t, :], fstat[:, t, :]).then_inc(mv_ready.sem, 1)

                def first_stats(g, j):
                    statistics(g * JT + j)

                def norm(k, g, j):
                    t = g * JT + j
                    n = k * TILES + t + 1
                    dve.wait_ge(mv_ready.sem, mv_ready.value(i, n))
                    dve.wait_ge(rstd_ready.sem, rstd_ready.value(i, n))
                    dve.tensor_scalar(xn[:, t, 0:D], tile_of(t), mv[:, t, 0:1], rstd[:, t:t + 1], ALU.subtract,
                                      ALU.mult).then_inc(xn_ready.sem, 1)

                def shift(n):
                    dve.wait_ge(s_done.sem, s_done.value(i, n + 1))
                    scores = ps_s[:, :].rearrange("p (h s) -> p h s", h=H)
                    link(i, dve.tensor_reduce(smax[:, :], scores, AX_X, ALU.max))
                    if n:
                        dve.wait_ge(exp_done.sem, exp_done.value(i, n))
                    dve.tensor_tensor(shifted.rearrange("p (h s) -> p h s", h=H), scores,
                                      smax[:, :].unsqueeze(2).to_broadcast([P, H, S]), ALU.subtract).then_inc(sub_done.sem, 1)

                def values(n):
                    dve.wait_ge(pv_done.sem, pv_done.value(i, n + 1))
                    sums = ps_o[:, 0:PAIRS * VW].rearrange("p (h w) -> p h w", h=H)
                    link(i, dve.reciprocal(rsum[:, :], sums[:, :, E]))
                    dve.tensor_tensor(onorm[:, :].rearrange("p (h e) -> p h e", h=H), sums[:, :, 0:E],
                                      rsum[:, :].unsqueeze(2).to_broadcast([P, H, E]), ALU.mult).then_inc(on_done.sem, 1)

                def project(n):
                    t = n % ATT
                    dve.wait_ge(pr_done.sem, pr_done.value(i, n + 1))
                    dve.tensor_tensor(tile_of(t), tile_of(t), ps_w[:, 0:D], ALU.add).then_inc(x_done.sem, 1)
                    dve.wait_ge(x_done.sem, x_done.value(i, ADDED["project", n] + 1))
                    statistics(t)

                def mix(g):
                    for w in range(2):
                        for c in range(C):
                            dve.wait_ge(prev_done.sem, prev_done.value(i, (g * 2 + w) * C + c + 1))
                            mu = (MU_K, MU_R)[w] + c
                            dve.scalar_tensor_tensor(out=mixed(w, g, c), in0=xnT[:, g, c, 1:L + 1], scalar=cols[:, mu:mu + 1],
                                                     in1=mixed(w, g, c), op0=ALU.mult, op1=ALU.add).then_inc(mix_done.sem, 1)

                def key(g):
                    for c in range(C):
                        dve.wait_ge(relu_done.sem, relu_done.value(i, g * C + c + 1))
                        dve.tensor_tensor(kact(g, c), kact(g, c), kact(g, c), ALU.mult).then_inc(kact_done.sem, 1)

                def value(g, j):
                    t = g * JT + j
                    dve.wait_ge(val_done.sem, val_done.value(i, t + 1))
                    dve.wait_ge(gate_done.sem, gate_done.value(i, g * 2 + j // 2 + 1))
                    link(i, dve.scalar_tensor_tensor(out=gated, in0=gate_of(g, j // 2)[:, j % 2 * D:(j % 2 + 1) * D], scalar=1.0,
                                                     in1=(ps_w, ps_o)[j % 2][:, 0:D], op0=ALU.add, op1=ALU.mult))
                    dve.scalar_tensor_tensor(out=tile_of(t), in0=gated, scalar=0.5, in1=tile_of(t),
                                             op0=ALU.mult, op1=ALU.add).then_inc(x_done.sem, 1)
                    dve.wait_ge(x_done.sem, x_done.value(i, ADDED["value", g, j] + 1))
                    statistics(t)

                def spread(a):
                    return a.unsqueeze(2).to_broadcast([P, TILES, X])

                def along(a):
                    return a.unsqueeze(1).to_broadcast([P, TILES, X])

                def pick(p, top, first, hot, t1, t2):
                    link(i, dve.tensor_reduce(r1[:, top], r8[:, p], AX_X, ALU.max))
                    link(i, dve.tensor_tensor(r8[:, t1], r8[:, p], spread(r1[:, top]), ALU.is_equal))
                    link(i, dve.scalar_tensor_tensor(out=r8[:, t2], in0=r8[:, t1], scalar=float(-X),
                                                     in1=along(iota8[:, :]), op0=ALU.mult, op1=ALU.add))
                    link(i, dve.tensor_reduce(r1[:, first], r8[:, t2], AX_X, ALU.min))
                    link(i, dve.tensor_tensor(r8[:, hot], along(iota8m[:, :]), spread(r1[:, first]), ALU.is_equal))

                def choose():
                    dve.wait_ge(turn_read.sem, turn_read.value(i, TURN["logits",] + 1))
                    link(i, dve.tensor_reduce(r1[:, 0], r8[:, 10], AX_X, ALU.max))
                    dve.tensor_tensor(r8[:, 0], r8[:, 10], spread(r1[:, 0]), ALU.subtract).then_inc(lsub_done.sem, 1)
                    dve.wait_ge(lexp_done.sem, lexp_done.value(i, 1))
                    link(i, dve.tensor_reduce(r1[:, 1], r8[:, 1], AX_X, ALU.add))
                    link(i, dve.reciprocal(r1[:, 2], r1[:, 1]))
                    link(i, dve.tensor_tensor(r8[:, 2], r8[:, 1], spread(r1[:, 2]), ALU.mult))
                    pick(2, 3, 4, 3, 4, 5)
                    link(i, dve.scalar_tensor_tensor(out=r8[:, 6], in0=r8[:, 3], scalar=-2.0, in1=r8[:, 2],
                                                     op0=ALU.mult, op1=ALU.add))
                    pick(6, 5, 8, 7, 4, 5)
                    dve.tensor_tensor(chosen[:, :, :], r8[:, 3], r8[:, 7], ALU.add).then_inc(chosen_done.sem, 1)
                    dve.tensor_tensor(r1[:, 6], r1[:, 5], r1[:, 3], ALU.subtract).then_inc(gap_done.sem, 1)
                    dve.wait_ge(gexp_done.sem, gexp_done.value(i, 1))
                    link(i, dve.tensor_scalar(r1[:, 8], r1[:, 7], 1.0, None, ALU.add))
                    link(i, dve.reciprocal(r1[:, 9], r1[:, 8]))
                    mark(dve.tensor_copy(xn[:, :, W1ST], r1[:, 9]))
                    mark(dve.tensor_tensor(xn[:, :, W2ND], r1[:, 9], r1[:, 7], ALU.mult))
                    mark(dve.tensor_scalar(xn[:, :, FIRST], r1[:, 4], float(X), None, ALU.add))
                    mark(dve.tensor_copy(xn[:, :, TOKEN], token[:, bass.ds(i * TILES, TILES)]))

                def places():
                    dve.wait_ge(turn_read.sem, turn_read.value(i, TURN["ranks",] + 1))
                    for t in range(TILES):
                        mark(dve.tensor_tensor(r8[:, 8, t], ranks[:, 0, t], count[:, :], ALU.add))
                        link(i, dve.tensor_tensor(count[:, :], ranks[:, 1, t], count[:, :], ALU.add))
                    link(i, dve.tensor_tensor(r8[:, 9], r8[:, 8], along(region[:, :]), ALU.add))
                    for k in range(2):
                        link(i, dve.tensor_tensor(r8[:, 4 + k], r8[:, 9], r8[:, 3 + 4 * k], ALU.mult))
                        link(i, dve.tensor_reduce(r1[:, 3 + k], r8[:, 4 + k], AX_X, ALU.add))
                        link(i, dve.tensor_copy(where_[:, k, :], r1[:, 3 + k]))
                    dve.sem_inc(packed_done.sem, 1)

                stage_of({"first_stats": first_stats, "norm": norm, "shift": shift, "values": values, "project": project,
                          "mix": mix, "key": key, "value": value, "choose": choose, "places": places})
                assert links[0] == DVE_STEPS, links[0]

            done[0] = 0

            def tstep(ins):
                done[0] += 1
                ins.then_inc(tab_step, 1)
                dve.wait_ge(tab_step, done[0])

            def over_slots(a):
                return a.unsqueeze(1).to_broadcast([P, SLOTS, X])

            tstep(dve.tensor_scalar(tt[:, 0, :], count[:, :], float(P - 1), None, ALU.add))
            tstep(dve.tensor_copy(tti[:, :], tt[:, 0, :]))
            tstep(dve.tensor_scalar(tti[:, :], tti[:, :], 7, None, ALU.logical_shift_right))
            tstep(dve.tensor_copy(tt[:, 1, :], tti[:, :]))
            tstep(dve.memset(tt[:, 2, :], 1.0))
            tstep(dve.tensor_tensor_scan(tt[:, 3, :], tt[:, 2, :], tt[:, 1, :], 0.0, ALU.mult, ALU.add))
            tstep(dve.tensor_tensor(ge, iota_s[:, :].unsqueeze(2).to_broadcast([P, SLOTS, X]),
                                    over_slots(tt[:, 3, :]), ALU.is_ge))
            tstep(dve.tensor_reduce(st[:, 0, :], ge, AX_X, ALU.add))
            tstep(dve.tensor_tensor(gen, ge, over_slots(tt[:, 1, :]), ALU.mult))
            tstep(dve.tensor_reduce(st[:, 1, :], gen, AX_X, ALU.add))
            tstep(dve.tensor_tensor(st[:, 2, :], iota_s[:, :], st[:, 1, :], ALU.subtract))
            tstep(dve.scalar_tensor_tensor(out=st[:, 3, :], in0=st[:, 0, :], scalar=float(REGION // P), in1=st[:, 2, :],
                                           op0=ALU.mult, op1=ALU.add))
            tstep(dve.tensor_scalar(st[:, 4, :], st[:, 0, :], float(X - 1), None, ALU.min))
            dve.tensor_scalar(slot_row[:, :], st[0:1, 3, :], float(P), None, ALU.mult).then_inc(tables, 1)
            dve.tensor_copy(slot_exp[:, :], st[0:1, 4, :]).then_inc(tables, 1)
            dve.sem_inc(ps_y_free, 1)
            dve.sem_inc(ysb_free, 1)

            def column(a, s, k):
                return a[:, bass.ds(s, 1), k:k + 1].rearrange("p s w -> p (s w)")

            def take(s, n_loaded):
                dve.wait_ge(xg_loaded, n_loaded)
                dve.tensor_copy(slot_cols[:, bass.ds(s, 1), :].rearrange("p s w -> p (s w)"),
                                xg[:, D:RW]).then_inc(wi_out, 1)

            def copy_hidden(s):
                dve.wait_ge(ht_done, s + 1)
                for half in range(2):
                    dve.tensor_copy(hidT[:, 4 * half:4 * half + 4, :].rearrange("p k t -> p (k t)"),
                                    ps_p[:, half * 512:(half + 1) * 512]).then_inc(ht_out, 1)

            TABS = done[0]
            SLOT_STEPS = 4

            def weigh(s):
                dve.wait_ge(wi_out, s + 1)
                expert = st[:, 4, bass.ds(s, 1)]
                for k, (col, test) in enumerate([(0, ALU.is_equal), (1, ALU.not_equal)]):
                    dve.tensor_scalar(column(slot_w, s, k), column(slot_cols, s, FIRST - D), expert,
                                      column(slot_cols, s, col), test, ALU.mult).then_inc(tab_step, 1)
                dve.wait_ge(tab_step, SLOT_STEPS * s + (TABS + 2))
                dve.tensor_tensor(column(slot_w, s, 2), column(slot_w, s, 0), column(slot_w, s, 1), ALU.add).then_inc(tab_step, 1)
                dve.wait_ge(ysb_free, s + 1)
                dve.tensor_copy(slot_tok[:, :], column(slot_cols, s, TOKEN - D)).then_inc(tab_step, 1)
                dve.wait_ge(tab_step, SLOT_STEPS * s + (TABS + 4))
                dve.wait_ge(y_done, s + 1)
                dve.tensor_scalar(ysb[:, :], ps_w[:, 0:D], column(slot_w, s, 2), None, ALU.mult).then_inc(ps_y_free, 1)
                dve.wait_ge(ps_y_free, s + 2)
                dve.sem_inc(tok_out, 1)

            take(0, 16)
            take(1, 32)
            with dve.Fori(0, SLOTS - 2) as s:
                copy_hidden(s)
                weigh(s)
                take(s + 2, 16 * s + 48)
            for s in (SLOTS - 2, SLOTS - 1):
                copy_hidden(s)
                weigh(s)


def kernel(**inputs):
    import numpy as np
    import concourse.bacc as bacc
    from concourse.bass_utils import run_bass_kernel_spmd

    def get(name):
        return np.ascontiguousarray(inputs[name])

    ctx = get("ctx_1024").transpose(2, 0, 1)
    ctx = np.ascontiguousarray(np.concatenate([ctx, ctx], axis=2)).reshape(D, B * 2 * S)
    names = ["L0_xcond_Wq", "L0_xcond_Wk", "L0_xcond_Wv", "L0_xcond_Wo", "L0_ffn_W_r", "L0_ffn_W_k", "L0_ffn_W_v",
             "L1_xcond_Wq", "L1_xcond_Wk", "L1_xcond_Wv", "L1_xcond_Wo"]
    mats = np.ascontiguousarray(np.stack([get(n).T for n in names]))
    by_col = ["L0_xcond_bq", "L0_xcond_bk", "L1_xcond_bq", "L1_xcond_bk", "L0_ffn_mu_r", "L0_ffn_mu_k"]
    cols = np.ascontiguousarray(np.concatenate([get(n).reshape(C, P) for n in by_col]).T)
    by_row = ["fside_BxS2_0", "L0_xcond_bo", "L1_xcond_bo", "L0_xcond_bv", "L1_xcond_bv", "L1_ffn_b1", "L1_ffn_b2", "L1_ffn_br"]
    vecs = np.concatenate([get(n).reshape(-1) for n in by_row])
    vecs = np.concatenate([vecs, np.zeros(VECS - vecs.size, vecs.dtype)])
    arrays = {
        "in_x": get("x").reshape(B * L, D), "in_ctx": ctx, "in_tau": get("condB_tau"), "in_mats": mats, "in_cols": cols,
        "in_vecs": vecs, "in_w1": get("L1_ffn_W1"), "in_w2": get("L1_ffn_W2"), "in_wr": get("L1_ffn_Wr"),
    }
    nc = bacc.Bacc("TRN2", target_bir_lowering=False, num_devices=1)
    args = [nc.dram_tensor(n, a.shape, mybir.dt.from_np(a.dtype), kind="ExternalInput").ap() for n, a in arrays.items()]
    args.append(nc.dram_tensor("out_x", (B * L + P, D), F32, kind="ExternalOutput").ap())
    build(nc, *args)
    r = run_bass_kernel_spmd(nc, [arrays], core_ids=[0])
    return r.results[0]["out_x"][0:B * L].reshape(B, L, D)
```

```python
from contextlib import ExitStack

import concourse.bass as bass
from concourse import mybir

F32, BF16 = mybir.dt.float32, mybir.dt.bfloat16
I32, U32 = mybir.dt.int32, mybir.dt.uint32
ALU = mybir.AluOpType
ACT = mybir.ActivationFunctionType
AX_X = mybir.AxisListType.X

P = 128
B, L, S, D = 4, 512, 64, 256
H, E = 16, 16
C = D // P
JT = L // P
NT = B * JT
G = H // C
PAIRS = H // 2
VW = 2 * (E + 1)
X, FF = 8, 1024
KF = FF // P
EPS = 1e-5

REGION = B * L
SLOTS = (2 * B * L - X) // P + X
SPARE = SLOTS - 2 * B * L // P
ROWS = X * REGION + SPARE * P
RW = D + 4
W1ST, W2ND, FIRST, TOKEN = range(D, RW)

PAIR = 2
TILES = PAIR * JT
HALVES = JT // 2
ATT = PAIR * JT

WK, WV, WQ, WO = (0, 1), (2, 3), (4, 5), (6, 7)
FR, FK, FV = 8, 9, 10
MATS = 11
FIRST_MATS = 5

DELTA = 0
BO = (B * S, B * S + D)
BV = (BO[1] + D, BO[1] + 2 * D)
B2 = BV[1] + D
BR = B2 + X * D
VECW = -(-(BR + X) // P)
VECS = VECW * P
BQ, BK, MU_R, MU_K = (0, 4), (2, 6), 8, 10
B1 = 12
COLS = B1 + X * KF


def order_of_stages():
    out = []

    def turns(k, g):
        return [("turn", k, g, h) for h in range(HALVES)]

    def norms(k, g):
        return [("norm", k, g, j) for j in range(JT)]

    def attention(l, early, start, between):
        first, last = l * ATT, (l + 1) * ATT - 1
        out.extend([("scores", first), ("shift", first)] + early + [("exp", first)] + start)
        for n in range(first, last + 1):
            out.append(("turn_probs", n))
            if n > first + 1:
                out.append(("norm", 2 * l + 1, (n - 2 - first) // JT, (n - 2 - first) % JT))
            if n > first:
                out.append(("turn_out", n - 1))
            if n < last:
                out.extend([("scores", n + 1), ("shift", n + 1), ("exp", n + 1)])
            else:
                out.extend(between.get(-1, []))
            out.append(("values", n))
            if n > first:
                out.append(("project", n - 1))
            out.extend(between.get(n - first, []))
        out.extend([("turn_out", last)] + between.get(ATT, []) + [("project", last)])
        out.extend(("norm", 2 * l + 1, PAIR - 1, j) for j in (JT - 2, JT - 1))

    out.extend(norms(0, 0) + turns(0, 0) + [("queries", 0, 0), ("keys", 0, 0), ("keys", 0, 1)] + norms(0, 1))
    attention(0, turns(0, 1), [("queries", 0, 1)],
              {JT: [("turn", 1, 0, 0)], JT + 1: [("turn", 1, 0, 1), ("before", 0)], JT + 2: [("mix", 0, 0), ("mix", 0, 1)],
               -1: [("key", 0), ("square", 0)], ATT: [("gate", 0)]})
    out.extend([("value", 0, 0)] + turns(1, 1) + [("before", 1), ("mix", 1, 0), ("value", 0, 1), ("key", 1), ("mix", 1, 1)])
    out.extend(norms(2, 0) + [("square", 1)] + turns(2, 0) + [("keys", 1, 0), ("queries", 1, 0), ("gate", 1)])
    attention(1, [], [("value", 1, 0), ("norm", 2, 1, 0), ("norm", 2, 1, 1), ("value", 1, 1), ("norm", 2, 1, 2), ("norm", 2, 1, 3)], {0: [("keys", 1, 1), ("turn", 2, 1, 0)], 1: [("turn", 2, 1, 1), ("queries", 1, 1)],
                        JT: [("turn", 3, 0, 0)], JT + 1: [("turn", 3, 0, 1), ("logits", 0), ("choose", 0, 0)],
                        JT + 2: [("choose", 0, 1)], JT + 3: [("choose", 0, 2)], ATT: [("ranks", 0), ("choose", 0, 3)]})
    out.extend(turns(3, 1) + [("places", 0), ("logits", 1)] + [("scatter", 0, j) for j in range(JT)])
    out.extend([("choose", 1, part) for part in range(3)] + [("ranks", 1), ("choose", 1, 3), ("places", 1)])
    out.extend(("scatter", 1, j) for j in range(JT))
    return out


ORDER = order_of_stages()
TURN = {s: n for n, s in enumerate(x for x in ORDER if x[0] in ("turn", "turn_out", "logits", "ranks"))}
ADDED = {}
for s in ORDER:
    if s[0] in ("project", "value"):
        ADDED[s] = max(ADDED.values(), default=0) + {"project": 1, "value": 2}[s[0]]


class Signal:

    def __init__(self, sem, per):
        self.sem, self.per = sem, per

    def value(self, i, k):
        return i * self.per + k


def build(nc, x_in, ctx_in, tau_in, mats_in, cols_in, vecs_in, w1_in, w2_in, wr_in, out):
    routed = nc.dram_tensor("routed_rows", (ROWS, RW), F32, kind="Internal").ap()
    stack = ExitStack()
    with stack:
        def sb(name, shape, dt=F32):
            return stack.enter_context(nc.sbuf_tensor(name, shape, dt))

        def pb(name, width):
            return stack.enter_context(nc.psum_tensor(name, [P, width], F32))

        def sem(name):
            return stack.enter_context(nc.semaphore(name))

        def signal(name, per):
            return Signal(sem(name), per)

        EW = C * FF + KF * D
        EARLY = 4
        experts = sb("experts", [P, X * EW])
        room = [EARLY * EW]

        def lent(*dims):
            n = 1
            for d in dims:
                n *= d
            a = experts[:, room[0]:room[0] + n]
            room[0] += n
            assert room[0] <= X * EW
            names = "abcd"[:len(dims)]
            if len(dims) > 1:
                kw = {names[i]: dims[i] for i in range(1, len(dims))}
                a = a.rearrange(f"p ({' '.join(names)}) -> p {' '.join(names)}", **kw)
            return a

        vbd = lent(2 * B * PAIRS, VW)
        keys = lent(2 * C, B * S)
        mats = lent(MATS * C, D)
        kbd = lent(PAIR, C, G * S)
        shifted = lent(L * C)
        assert room[0] <= (X - 1) * EW
        qT = lent(PAIR, C, L)
        xnT = lent(PAIR, C, L + 1)

        def mat(m, c):
            return mats[:, m * C + c, :]

        x = sb("x", [P, NT, D])
        rows3 = sb("rows3", [3, VECS], BF16)
        xn = sb("xn", [P, TILES, RW])
        probs = sb("probs", [P, H * S])
        probsT = sb("probsT", [P, PAIRS, P])
        onorm = sb("onorm", [P, D])
        oT = sb("oT", [P, 2, C, P])
        gated = [oT[:, m, :, :].rearrange("p c t -> p (c t)") for m in range(2)]
        ident = sb("ident", [P, P])
        tri = sb("tri", [P, P], BF16)
        ones = sb("ones", [P, P], BF16)
        ones3 = ones[0:3, :]
        quarter = sb("quarter", [3, P], BF16)
        mask = sb("mask", [P, G])
        cols = sb("cols", [P, COLS])
        omu = sb("omu", [P, 4])
        wr = sb("wr", [P, C, X])
        tau = sb("tau", [P, B])
        halfneg = sb("halfneg", [P, 1])
        fstat = sb("fstat", [P, TILES, 6])
        mv = sb("mv", [P, TILES, 2])
        veps = sb("veps", [P, TILES])
        rstd = sb("rstd", [P, TILES])
        fstat0 = sb("fstat0", [P, NT, 6])
        mv0 = sb("mv0", [P, NT, 2])
        rstd0 = sb("rstd0", [P, NT])
        smax = sb("smax", [P, H])
        rsum = sb("rsum", [P, H])
        r8 = sb("r8", [P, PAIR, 11, JT, X])
        r1 = sb("r1", [P, PAIR, 10, JT])
        ranks = sb("ranks", [P, PAIR, 2, JT, X])
        chosen = sb("chosen", [P, TILES, X], BF16)
        iota8 = sb("iota8", [P, X])
        iota8m = sb("iota8m", [P, X])
        region = sb("region", [P, X])
        token = sb("token", [P, NT])
        count = sb("count", [P, X])
        where_ = sb("where", [P, 2, TILES], U32)
        vecs = sb("vecs", [P, VECW])
        vres = sb("vres", [P, 2, VECW])
        vpart = sb("vpart", [P, 3, VECW], BF16)
        ctxT = probs[:, :].rearrange("p (c b s) -> p c b s", c=C, b=B)

        QUARTERS = 4
        QK = KF // QUARTERS

        def hidden_chunk(k):
            q, at = k // QK, k % QK * P
            return (ps_s, ps_p)[q // 2][:, q % 2 * 512 + at:q % 2 * 512 + at + P]

        xg = xn[:, 0, :]
        xgT = oT[:, 0, :, :]
        hidT = probsT
        w1s = x[:, 0:C * FF // D, :].rearrange("p t d -> p (t d)").rearrange("p (c f) -> p c f", c=C)
        ysb = onorm
        empty = sb("empty", [P, RW])
        slot_cols = sb("slot_cols", [P, SLOTS, RW - D])
        slot_w = sb("slot_w", [P, SLOTS, 3])
        slot_tok = sb("slot_tok", [P, 1], U32)
        iota_s = sb("iota_s", [P, SLOTS])
        ge = probs[:, 0:SLOTS * X].rearrange("p (s e) -> p s e", e=X)
        gen = probs[:, SLOTS * X:2 * SLOTS * X].rearrange("p (s e) -> p s e", e=X)
        tt = sb("tt", [P, 4, X])
        tti = sb("tti", [P, X], I32)
        st = sb("st", [P, 5, SLOTS])
        slot_row = sb("slot_row", [1, SLOTS], I32)
        slot_exp = sb("slot_exp", [1, SLOTS], I32)

        ps_t = [pb("ps_t0", 512), pb("ps_t1", 512)]
        ps_s = pb("ps_s", 1024)
        ps_p = pb("ps_p", 1024)
        ps_o = pb("ps_o", 512)
        ps_w = pb("ps_w", 512)

        ld_ctx, ld_mats, ld_more, ld_small, ld_vecs = (sem(n) for n in ("ld_ctx", "ld_mats", "ld_more", "ld_small", "ld_vecs"))
        ld_wr = sem("ld_wr")
        ld_x = [sem(f"ld_x{i}") for i in range(B // PAIR)]
        ld_rows3, ld_fill, ld_early, ld_late, ld_last = (sem(n) for n in ("ld_rows3", "ld_fill", "ld_early", "ld_late", "ld_last"))
        mv0_ready, rstd0_ready = sem("mv0_ready"), sem("rstd0_ready")
        const_ready = sem("const_ready")
        const_step = sem("const_step")
        split_ready = sem("split_ready")
        pre_step = sem("pre_step")
        pre_mm = sem("pre_mm")
        pre_ev = sem("pre_ev")

        DVE_STEPS = 144
        dve_step = signal("dve_step", DVE_STEPS)
        pool_step = signal("pool_step", 24)
        mv_ready = signal("mv_ready", 24)
        rstd_ready = signal("rstd_ready", 24)
        xn_ready = signal("xn_ready", 32)
        turned = signal("turned", len(TURN))
        turn_read = signal("turn_read", len(TURN))
        q_done = signal("q_done", 2 * PAIR * C)
        q_out = signal("q_out", 2 * PAIR * C)
        kbd_ready = signal("kbd_ready", 2 * PAIR * C)
        s_done = signal("s_done", 2 * ATT * C)
        sub_done = signal("sub_done", 2 * ATT * C)
        exp_done = signal("exp_done", 2 * ATT * C)
        pt_done = signal("pt_done", 2 * ATT * C)
        pt_out = signal("pt_out", 2 * ATT * C)
        pv_done = signal("pv_done", 2 * ATT)
        on_done = signal("on_done", 2 * ATT)
        pr_done = signal("pr_done", 2 * ATT)
        x_done = signal("x_done", max(ADDED.values()))
        prev_done = signal("prev_done", PAIR * 2 * C)
        mixk_done = signal("mixk_done", PAIR * C)
        mixr_done = signal("mixr_done", PAIR * C)
        key_done = signal("key_done", PAIR * C)
        relu_done = signal("relu_done", PAIR * C)
        kact_done = signal("kact_done", PAIR * C)
        rg_done = signal("rg_done", PAIR * 2)
        gate_done = signal("gate_done", PAIR * 2)
        val_done = signal("val_done", PAIR * JT)
        gated_done = signal("gated_done", PAIR * JT)
        lsub_done = signal("lsub_done", PAIR)
        lexp_done = signal("lexp_done", PAIR)
        gap_done = signal("gap_done", PAIR)
        gexp_done = signal("gexp_done", PAIR)
        chosen_done = signal("chosen_done", PAIR)
        packed_done = signal("packed_done", PAIR)
        rows_free = [sem(f"rows_free{g}") for g in range(PAIR)]
        scattered = [signal(f"scattered{g}", 16 * 2 * JT) for g in range(PAIR)]
        passed = sem("passed")
        xout = sem("xout")

        tab_step = sem("tab_step")
        tables = sem("tables")
        xg_loaded = sem("xg_loaded")
        wi_out = sem("wi_out")
        xt_done = sem("xt_done")
        xt_out = sem("xt_out")
        w1_ready = sem("w1_ready")
        hid_done = sem("hid_done")
        gelu_done = sem("gelu_done")
        y_part = sem("y_part")
        ps_y_free = sem("ps_y_free")
        tok_out = sem("tok_out")
        ysb_free = sem("ysb_free")
        added = sem("added")

        PRE_KEYS = 2 * C * B
        PRE_VALS = 2 * B * 2

        def mixed(w, g, c):
            return (qT, kbd)[w][:, g, c, :]

        def kact(g, c):
            return xnT[:, g, c, 1:L + 1]

        def gate_of(g, half):
            return qT[:, g, half, :]

        def stage_of(own):
            for stage, *which in ORDER:
                if stage in own:
                    own[stage](*which)

        def load_expert(eng, e, done):
            at = e * EW
            eng.dma_start(experts[:, at:at + C * FF].rearrange("p (c f) -> p c f", c=C),
                          w1_in[e].rearrange("(c p) f -> p c f", p=P)).then_inc(done, 16)
            eng.dma_start(experts[:, at + C * FF:at + EW].rearrange("p (k d) -> p k d", k=KF),
                          w2_in[e].rearrange("(k p) d -> p k d", p=P)).then_inc(done, 16)

        block = stack.enter_context(nc.Block())

        @block.sync
        def _(sp):
            sp.dma_start(ctxT, ctx_in.rearrange("(c p) (b s) -> p c b s", p=P, b=B)).then_inc(ld_ctx, 16)
            src = mats_in.rearrange("m (c p) n -> p (m c) n", p=P)
            x_tiles = x_in.rearrange("(t p) d -> p t d", p=P)
            sp.dma_start(x[:, 0:TILES, :], x_tiles[:, 0:TILES, :]).then_inc(ld_x[0], 16)
            sp.dma_start(mats[:, 0:FIRST_MATS * C, :], src[:, 0:FIRST_MATS * C, :]).then_inc(ld_mats, 16)
            sp.dma_start(mats[:, FIRST_MATS * C:, :], src[:, FIRST_MATS * C:, :]).then_inc(ld_more, 16)
            sp.dma_start(x[:, TILES:NT, :], x_tiles[:, TILES:NT, :]).then_inc(ld_x[1], 16)
            sp.wait_ge(split_ready, 3)
            for i in range(3):
                sp.dma_start(rows3[i:i + 1, :].rearrange("o (p k) -> o p k", k=VECW), vpart[:, i, :]).then_inc(ld_rows3, 16)
            sp.wait_ge(const_ready, 1)
            sp.dma_start(routed.rearrange("(n p) k -> p n k", p=P),
                         empty[:, :].unsqueeze(1).to_broadcast([P, ROWS // P, RW])).then_inc(ld_fill, 16)
            for e in range(EARLY):
                load_expert(sp, e, ld_early)
            def write_out(i):
                sp.wait_ge(x_done.sem, x_done.value(i, x_done.per))
                sp.dma_start(out[0:B * L, :].rearrange("(t p) d -> p t d", p=P)[:, bass.ds(i * TILES, TILES), :],
                             x[:, bass.ds(i * TILES, TILES), :]).then_inc(xout, 16)

            with sp.Fori(0, B // PAIR - 1) as i:
                write_out(i)
                for g in range(PAIR):
                    sp.wait_ge(scattered[g].sem, scattered[g].value(i, scattered[g].per))
                    sp.sem_inc(rows_free[g], 1)
            write_out(B // PAIR - 1)
            for e in range(EARLY, X - 1):
                load_expert(sp, e, ld_late)
            sp.wait_ge(tables, 2)
            for done_ in scattered:
                sp.wait_ge(done_.sem, B // PAIR * done_.per)

            def load_slot(s):
                row = sp.value_load(slot_row[0:1, bass.ds(s, 1)], min_val=0, max_val=ROWS - P)
                sp.dma_start(xg, routed[bass.ds(row, P), :]).then_inc(xg_loaded, 16)

            def load_next_slot(s):
                sp.wait_ge(xt_done, s)
                sp.wait_ge(wi_out, s)
                load_slot(s)

            load_slot(0)
            load_next_slot(1)
            load_expert(sp, X - 1, ld_last)
            with sp.Fori(2, SLOTS) as s:
                load_next_slot(s)

        @block.gpsimd
        def _(pool):
            fill = empty[:, :]
            pool.memset(fill, 0.0).then_inc(const_step, 1)
            pool.wait_ge(const_step, 1)
            pool.iota(fill[:, TOKEN:TOKEN + 1], [[0, 1]], base=B * L, channel_multiplier=1,
                      allow_small_or_imprecise_dtypes=True).then_inc(const_ready, 1)
            pool.memset(ident[:, :], 0.0).then_inc(const_step, 1)
            pool.memset(tri[:, :], 1.0).then_inc(const_step, 1)
            pool.memset(mask[:, :], 1.0).then_inc(const_step, 1)
            pool.memset(ones[:, :], 1.0).then_inc(const_ready, 1)
            pool.memset(quarter[:, :], 0.25).then_inc(const_ready, 1)
            pool.memset(halfneg[:, :], -0.5).then_inc(const_step, 1)
            pool.memset(xnT[:, :, :, 0:1], 0.0).then_inc(const_ready, 1)
            pool.wait_ge(const_step, 5)
            pool.affine_select(out=ident[:, :], in_=ident[:, :], compare_op=ALU.not_equal, fill=1.0, base=0,
                               pattern=[[-1, P]], channel_multiplier=1).then_inc(const_ready, 1)
            pool.affine_select(out=tri[:, :], in_=tri[:, :], compare_op=ALU.is_gt, fill=0.0, base=0,
                               pattern=[[1, P]], channel_multiplier=-1).then_inc(const_ready, 1)
            pool.affine_select(out=mask[:, :], in_=mask[:, :], compare_op=ALU.is_ge, fill=0.0, base=0,
                               pattern=[[-E, G]], channel_multiplier=1).then_inc(const_step, 1)
            pool.wait_ge(const_step, 6)
            pool.affine_select(out=mask[:, :], in_=mask[:, :], compare_op=ALU.is_ge, fill=0.0, base=E - 1,
                               pattern=[[E, G]], channel_multiplier=-1).then_inc(const_step, 1)
            pool.iota(iota8[:, :], [[1, X]], base=0, channel_multiplier=0, allow_small_or_imprecise_dtypes=True).then_inc(const_ready, 1)
            pool.iota(iota8m[:, :], [[1, X]], base=-X, channel_multiplier=0, allow_small_or_imprecise_dtypes=True).then_inc(const_ready, 1)
            pool.iota(region[:, :], [[REGION, X]], base=0, channel_multiplier=0, allow_small_or_imprecise_dtypes=True).then_inc(const_ready, 1)
            pool.iota(iota_s[:, :], [[1, SLOTS]], base=0, channel_multiplier=0, allow_small_or_imprecise_dtypes=True).then_inc(const_ready, 1)
            pool.iota(token[:, :], [[P, NT]], base=0, channel_multiplier=1, allow_small_or_imprecise_dtypes=True).then_inc(const_ready, 1)
            pool.wait_ge(const_step, 7)

            for free in rows_free:
                pool.sem_inc(free, 1)
            for i in range(B // PAIR):
                at = slice(i * TILES, (i + 1) * TILES)
                pool.wait_ge(mv0_ready, (i + 1) * TILES)
                pool.tensor_scalar(rstd0[:, at], mv0[:, at, 1], EPS, None, ALU.add).then_inc(const_step, 1)
                pool.wait_ge(const_step, 8 + i)
                pool.tensor_tensor(rstd0[:, at], rstd0[:, at], halfneg[:, :].to_broadcast([P, TILES]), ALU.pow).then_inc(rstd0_ready, 1)
            pool.wait_ge(pre_ev, PRE_KEYS)
            with pool.Fori(0, B // PAIR) as i:
                def norm(k, g, j):
                    if k == 0:
                        return
                    t = g * JT + j
                    n = (k - 1) * TILES + t + 1
                    pool.wait_ge(mv_ready.sem, mv_ready.value(i, n))
                    pool.sem_inc(passed, 1)
                    pool.tensor_scalar(veps[:, t:t + 1], mv[:, t, 1:2], EPS, None, ALU.add).then_inc(pool_step.sem, 1)
                    pool.wait_ge(pool_step.sem, pool_step.value(i, n))
                    pool.tensor_tensor(rstd[:, t:t + 1], veps[:, t:t + 1], halfneg[:, :], ALU.pow).then_inc(rstd_ready.sem, 1)

                def block_diagonal_keys(l, g):
                    if l == 1:
                        pool.wait_ge(rg_done.sem, rg_done.value(i, 2 * (g + 1)))
                    for c in range(C):
                        pool.tensor_tensor(
                            kbd[:, g, c, :].rearrange("p (h s) -> p h s", h=G),
                            keys[:, l * C + c, bass.ds((i * PAIR + g) * S, S)].unsqueeze(1).to_broadcast([P, G, S]),
                            mask[:, :].unsqueeze(2).to_broadcast([P, G, S]), ALU.mult).then_inc(kbd_ready.sem, 1)

                def scatter(g, j):
                    if j == 0:
                        pool.wait_ge(packed_done.sem, packed_done.value(i, g + 1))
                        pool.sem_inc(passed, 1)
                        pool.wait_ge(ld_fill, 16)
                    t = g * JT + j
                    for k in range(2):
                        pool.indirect_dma_start(
                            out=routed, out_offset=bass.IndirectOffsetOnAxis(ap=where_[:, k, t:t + 1], axis=0),
                            in_=xn[:, t, :], in_offset=None).then_inc(scattered[g].sem, 16)

                stage_of({"norm": norm, "keys": block_diagonal_keys, "scatter": scatter})

            pool.wait_ge(xout, 16 * (B // PAIR + 1))

            with pool.Fori(0, SLOTS) as s:
                pool.wait_ge(tok_out, s + 1)
                pool.sem_inc(passed, 1)
                pool.indirect_dma_start(out=out, out_offset=bass.IndirectOffsetOnAxis(ap=slot_tok[:, 0:1], axis=0),
                                        in_=ysb[:, :], in_offset=None, compute_op=ALU.add).then_inc(added, 16)
                pool.wait_ge(added, 16 * s + 16)
                pool.sem_inc(ysb_free, 1)

        @block.scalar
        def _(act):
            act.dma_start(vecs[:, :], vecs_in.rearrange("(p k) -> p k", k=VECW)).then_inc(ld_vecs, 16)
            act.dma_start(cols[:, :], cols_in).then_inc(ld_small, 16)
            act.dma_start(tau[:, :], tau_in.rearrange("(o b) -> o b", o=1).partition_broadcast(P).rearrange("p o b -> p (o b)")).then_inc(ld_small, 16)
            act.dma_start(wr[:, :, :], wr_in.rearrange("(c p) e -> p c e", p=P)).then_inc(ld_wr, 16)
            act.wait_ge(const_ready, 1)
            act.dma_start(out[B * L:B * L + P, :], empty[:, 0:D]).then_inc(xout, 16)

            act.wait_ge(ld_small, 32)
            act.wait_ge(pre_step, 2 + 2 + TILES + 1)
            with act.Fori(0, B // PAIR) as i:
                def copy_turned(n, to, width):
                    act.wait_ge(turned.sem, turned.value(i, n + 1))
                    act.activation(to, ps_t[n % 2][:, 0:width], ACT.Copy).then_inc(turn_read.sem, 1)

                def turn(k, g, h):
                    copy_turned(TURN["turn", k, g, h], xnT[:, g, :, 1 + 2 * h * P:1 + 2 * (h + 1) * P], 2 * D)

                def turn_out(n):
                    copy_turned(TURN["turn_out", n], oT[:, n % 2, :, :], D)

                def queries(l, g):
                    for c in range(C):
                        n = (PAIR * l + g) * C + c + 1
                        act.wait_ge(q_done.sem, q_done.value(i, n))
                        act.activation(qT[:, g, c, :], (ps_w, ps_o)[c][:, :], ACT.Identity,
                                       bias=cols[:, BQ[l] + c:BQ[l] + c + 1]).then_inc(q_out.sem, 1)

                def exp(n):
                    for c in range(C):
                        act.wait_ge(sub_done.sem, sub_done.value(i, n * C + c + 1))
                        if n:
                            act.wait_ge(pt_done.sem, pt_done.value(i, (n - 1) * C + c + 1))
                        act.activation(probs[:, c * 512:(c + 1) * 512], shifted[:, c * 512:(c + 1) * 512],
                                       ACT.Exp).then_inc(exp_done.sem, 1)

                def turn_probs(n):
                    for c in range(C):
                        act.wait_ge(pt_done.sem, pt_done.value(i, n * C + c + 1))
                        if n:
                            act.wait_ge(pv_done.sem, pv_done.value(i, n))
                        act.activation(probsT[:, c * PAIRS // C:(c + 1) * PAIRS // C, :].rearrange("p a t -> p (a t)"),
                                       ps_p[:, c * 512:(c + 1) * 512], ACT.Copy).then_inc(pt_out.sem, 1)

                def before(g):
                    act.wait_ge(turn_read.sem, turn_read.value(i, TURN["turn", 1, g, HALVES - 1] + 1))
                    for w in range(2):
                        for c in range(C):
                            act.activation(mixed(w, g, c), xnT[:, g, c, 0:L], ACT.Copy,
                                           scale=omu[:, 2 * (1 - w) + c:2 * (1 - w) + c + 1]).then_inc(prev_done.sem, 1)

                def key(g):
                    for c in range(C):
                        act.wait_ge(key_done.sem, key_done.value(i, g * C + c + 1))
                        if c == 0:
                            act.wait_ge(mixk_done.sem, mixk_done.value(i, (g + 1) * C))
                            act.wait_ge(mixr_done.sem, mixr_done.value(i, (g + 1) * C))
                        act.activation(kact(g, c), ps_s[:, c * L:(c + 1) * L], ACT.Relu).then_inc(relu_done.sem, 1)

                def gate(g):
                    for half in range(2):
                        act.wait_ge(rg_done.sem, rg_done.value(i, g * 2 + half + 1))
                        act.activation(gate_of(g, half), ps_p[:, half * 512:(half + 1) * 512], ACT.Tanh,
                                       scale=0.5).then_inc(gate_done.sem, 1)

                def logits(g):
                    copy_turned(TURN["logits", g], r8[:, g, 10].rearrange("p t e -> p (t e)"), JT * X)

                def choose(g, part):
                    if part == 0:
                        act.wait_ge(lsub_done.sem, lsub_done.value(i, g + 1))
                        act.activation(r8[:, g, 1], r8[:, g, 0], ACT.Exp).then_inc(lexp_done.sem, 1)
                    elif part == 2:
                        act.wait_ge(gap_done.sem, gap_done.value(i, g + 1))
                        act.activation(r1[:, g, 7], r1[:, g, 6], ACT.Exp).then_inc(gexp_done.sem, 1)

                def ranked(g):
                    copy_turned(TURN["ranks", g], ranks[:, g].rearrange("p a t e -> p (a t e)"), 2 * JT * X)

                stage_of({"turn": turn, "turn_out": turn_out, "queries": queries, "exp": exp, "turn_probs": turn_probs,
                          "before": before, "key": key, "gate": gate, "logits": logits, "choose": choose,
                          "ranks": ranked})

            def xgT_out(n_done):
                act.wait_ge(xt_done, n_done)
                act.activation(xgT, ps_t[0][:, 0:D].rearrange("p (c t) -> p c t", c=C), ACT.Copy).then_inc(xt_out, 1)

            def gelu(s, first=False):
                e = act.value_load(slot_exp[0:1, bass.ds(s, 1)], min_val=0, max_val=X - 1)
                for k in range(KF):
                    if k % QK == 0:
                        act.wait_ge(hid_done, QUARTERS * s + (k // QK + 1))
                    if not first:
                        act.wait_ge(y_part, KF * s + (k + 1 - KF))
                    act.activation(hidT[:, k, :], hidden_chunk(k), ACT.Gelu,
                                   bias=cols[:, bass.ds(e * KF + (B1 + k), 1)]).then_inc(gelu_done, 1)

            act.wait_ge(tables, 2)
            xgT_out(1)
            xgT_out(2)
            gelu(0, first=True)
            with act.Fori(0, SLOTS - 2) as s:
                xgT_out(s + 3)
                gelu(s + 1)
            gelu(SLOTS - 1)

        @block.tensor
        def _(pe):
            pe.wait_ge(ld_ctx, 16)
            pe.wait_ge(ld_mats, 16)
            n = 0
            for l in range(2):
                for c in range(C):
                    bank = (ps_w, ps_o)[n % 2]
                    if n >= 2:
                        pe.wait_ge(pre_ev, B * (n - 1))
                    for k in range(C):
                        mm = pe.matmul(bank[:, 0:B * S], mat(WK[l], k)[:, c * P:(c + 1) * P], ctxT[:, k, :, 0:S],
                                       start=(k == 0), stop=(k == C - 1))
                    mm.then_inc(pre_mm, 1)
                    n += 1
            pe.wait_ge(const_ready, 5)
            pe.wait_ge(ld_rows3, 48)
            m = 0
            for l in range(2):
                for b in range(B):
                    bank = (ps_w, ps_o)[m % 2]
                    pe.wait_ge(pre_ev, PRE_KEYS - B + B * m if m < 2 else PRE_KEYS + 2 * (m - 1))
                    for k in range(C):
                        pe.matmul(bank[:, 0:D], ctxT[:, k, b, :], mat(WV[l], k), start=(k == 0), stop=False)
                    pe.matmul(bank[:, 0:D], ones3, rows3[:, BV[l]:BV[l] + D], start=False, stop=True).then_inc(pre_mm, 1)
                    m += 1
            pe.wait_ge(pre_ev, PRE_KEYS + PRE_VALS)
            pe.wait_ge(ld_more, 16)
            pe.wait_ge(ld_wr, 16)
            with pe.Fori(0, B // PAIR) as i:
                frees = {}

                def wait_free(bank):
                    if bank in frees:
                        signal_, n = frees[bank]
                        pe.wait_ge(signal_.sem, signal_.value(i, n))

                def turn_bank(n):
                    if n >= 2:
                        pe.wait_ge(turn_read.sem, turn_read.value(i, n - 1))
                    return ps_t[n % 2]

                def transposed(n, tiles):
                    bank = turn_bank(n)
                    for c in range(C):
                        for m, tile in enumerate(tiles):
                            at = (c * len(tiles) + m) * P
                            mm = pe.transpose(bank[:, at:at + P], tile[:, c * P:(c + 1) * P], ident[:, :])
                    mm.then_inc(turned.sem, 1)

                def turn(k, g, h):
                    pe.wait_ge(xn_ready.sem, xn_ready.value(i, k * TILES + g * JT + 2 * h + 2))
                    transposed(TURN["turn", k, g, h], [xn[:, g * JT + 2 * h + m, 0:D] for m in range(2)])

                def queries(l, g):
                    pe.wait_ge(turn_read.sem, turn_read.value(i, TURN["turn", 2 * l, g, HALVES - 1] + 1))
                    for c in range(C):
                        n = (PAIR * l + g) * C + c + 1
                        wait_free("wo"[c])
                        for k in range(C):
                            mm = pe.matmul((ps_w, ps_o)[c][:, :], mat(WQ[l], k)[:, c * P:(c + 1) * P],
                                           xnT[:, g, k, 1:L + 1], start=(k == 0), stop=(k == C - 1))
                        mm.then_inc(q_done.sem, 1)
                        frees["wo"[c]] = (q_out, n)

                def scores(n):
                    l, g, j = n // ATT, n % ATT // JT, n % JT
                    if j == 0:
                        pe.wait_ge(q_out.sem, q_out.value(i, (PAIR * l + g + 1) * C))
                        pe.wait_ge(kbd_ready.sem, kbd_ready.value(i, (PAIR * l + g + 1) * C))
                    if n == ATT:
                        pe.wait_ge(relu_done.sem, relu_done.value(i, PAIR * C))
                    for c in range(C):
                        if n:
                            pe.wait_ge(sub_done.sem, sub_done.value(i, (n - 1) * C + c + 1))
                        pe.matmul(ps_s[:, c * 512:(c + 1) * 512], qT[:, g, c, j * P:(j + 1) * P], kbd[:, g, c, :],
                                  start=True, stop=False)
                        pe.matmul(ps_s[:, c * 512:(c + 1) * 512].rearrange("p (h s) -> p h s", h=G), quarter[:, :],
                                  rows3[:, bass.ds((i * PAIR + g) * S + DELTA, S)].unsqueeze(1).to_broadcast([3, G, S]),
                                  start=False, stop=True).then_inc(s_done.sem, 1)

                def turn_probs(n):
                    if n == ATT:
                        pe.wait_ge(gate_done.sem, gate_done.value(i, PAIR * 2))
                    for c in range(C):
                        pe.wait_ge(exp_done.sem, exp_done.value(i, n * C + c + 1))
                        if n:
                            pe.wait_ge(pt_out.sem, pt_out.value(i, (n - 1) * C + c + 1))
                        for a in range(c * PAIRS // C, (c + 1) * PAIRS // C):
                            mm = pe.transpose(ps_p[:, a * P:(a + 1) * P], probs[:, a * P:(a + 1) * P], ident[:, :])
                        mm.then_inc(pt_done.sem, 1)

                def values(n):
                    l, g = n // ATT, n % ATT // JT
                    wait_free("o")
                    for a in range(PAIRS):
                        if a % (PAIRS // C) == 0:
                            pe.wait_ge(pt_out.sem, pt_out.value(i, n * C + a // (PAIRS // C) + 1))
                        mm = pe.matmul(ps_o[:, a * VW:(a + 1) * VW], probsT[:, a, :],
                                       vbd[:, bass.ds((i * PAIR + g) * PAIRS + (l * B * PAIRS + a), 1), :].rearrange("p a w -> p (a w)"),
                                       start=True, stop=True)
                    mm.then_inc(pv_done.sem, 1)
                    frees["o"] = (on_done, n + 1)

                def turn_out(n):
                    pe.wait_ge(on_done.sem, on_done.value(i, n + 1))
                    transposed(TURN["turn_out", n], [onorm])

                def project(n):
                    l = n // ATT
                    pe.wait_ge(turn_read.sem, turn_read.value(i, TURN["turn_out", n] + 1))
                    wait_free("w")
                    for k in range(C):
                        pe.matmul(ps_w[:, 0:D], oT[:, n % 2, k, :], mat(WO[l], k), start=(k == 0), stop=False)
                    pe.matmul(ps_w[:, 0:D], ones3, rows3[:, BO[l]:BO[l] + D], start=False, stop=True).then_inc(pr_done.sem, 1)
                    frees["w"] = (x_done, ADDED["project", n])

                def key(g):
                    pe.wait_ge(mixk_done.sem, mixk_done.value(i, (g + 1) * C))
                    if g == 0:
                        pe.wait_ge(sub_done.sem, sub_done.value(i, ATT * C))
                    else:
                        pe.wait_ge(relu_done.sem, relu_done.value(i, g * C))
                    for c in range(C):
                        for k in range(C):
                            mm = pe.matmul(ps_s[:, c * L:(c + 1) * L], mat(FK, k)[:, c * P:(c + 1) * P], mixed(0, g, k),
                                           start=(k == 0), stop=(k == C - 1))
                        mm.then_inc(key_done.sem, 1)

                def gate(g):
                    pe.wait_ge(mixr_done.sem, mixr_done.value(i, (g + 1) * C))
                    if g == 0:
                        pe.wait_ge(pt_out.sem, pt_out.value(i, ATT * C))
                    else:
                        pe.wait_ge(gate_done.sem, gate_done.value(i, g * 2))
                    for j in range(JT):
                        for k in range(C):
                            mm = pe.matmul(ps_p[:, j * D:(j + 1) * D], mixed(1, g, k)[:, j * P:(j + 1) * P], mat(FR, k),
                                           start=(k == 0), stop=(k == C - 1))
                        if j % 2:
                            mm.then_inc(rg_done.sem, 1)

                def value(g, h):
                    if h == 0:
                        pe.wait_ge(kact_done.sem, kact_done.value(i, (g + 1) * C))
                    for m in range(2):
                        j = 2 * h + m
                        wait_free("wo"[m])
                        for k in range(C):
                            mm = pe.matmul((ps_w, ps_o)[m][:, 0:D], kact(g, k)[:, j * P:(j + 1) * P], mat(FV, k),
                                           start=(k == 0), stop=(k == C - 1))
                        mm.then_inc(val_done.sem, 1)
                        frees["wo"[m]] = (gated_done, g * JT + j + 1)

                def logits(g):
                    n = TURN["logits", g]
                    bank = turn_bank(n)
                    pe.wait_ge(turn_read.sem, turn_read.value(i, TURN["turn", 3, g, HALVES - 1] + 1))
                    for t in range(JT):
                        to = bank[:, t * X:(t + 1) * X]
                        for k in range(C):
                            pe.matmul(to, xnT[:, g, k, 1 + t * P:1 + (t + 1) * P], wr[:, k, :], start=(k == 0), stop=False)
                        mm = pe.matmul(to, ones3, rows3[:, BR:BR + X], start=False, stop=True)
                    mm.then_inc(turned.sem, 1)

                def ranked(g):
                    bank = turn_bank(TURN["ranks", g])
                    pe.wait_ge(chosen_done.sem, chosen_done.value(i, g + 1))
                    picks = chosen[:, g * JT:(g + 1) * JT, :].rearrange("p t e -> p (t e)")
                    pe.matmul(bank[:, 0:JT * X], tri[:, :], picks, start=True, stop=True)
                    pe.matmul(bank[:, JT * X:2 * JT * X], ones[:, :], picks, start=True, stop=True).then_inc(turned.sem, 1)

                stage_of({"turn": turn, "queries": queries, "scores": scores, "turn_probs": turn_probs, "values": values,
                          "turn_out": turn_out, "project": project, "key": key, "gate": gate, "value": value,
                          "logits": logits, "ranks": ranked})

            def rows_transposed(n_loaded):
                pe.wait_ge(xg_loaded, n_loaded)
                for c in range(C):
                    mm = pe.transpose(ps_t[0][:, c * P:(c + 1) * P], xg[:, c * P:(c + 1) * P], ident[:, :])
                mm.then_inc(xt_done, 1)

            def hidden(s):
                pe.wait_ge(xt_out, s + 1)
                for k in range(KF):
                    if k % QK == 0:
                        pe.wait_ge(w1_ready, QUARTERS * s + (k // QK + 1))
                        if not (isinstance(s, int) and s == 0):
                            pe.wait_ge(gelu_done, KF * s + (k + QK - KF))
                    for c in range(C):
                        mm = pe.matmul(hidden_chunk(k), w1s[:, c, k * P:(k + 1) * P], xgT[:, c, :],
                                       start=(c == 0), stop=(c == C - 1))
                    if k % QK == QK - 1:
                        mm.then_inc(hid_done, 1)

            def result(s):
                e = pe.value_load(slot_exp[0:1, bass.ds(s, 1)], min_val=0, max_val=X - 1)
                pe.wait_ge(ps_y_free, s + 1)
                pe.matmul(ps_w[:, 0:D], ones3, rows3[:, bass.ds(e * D + B2, D)], start=True, stop=False)
                for k in range(KF):
                    pe.wait_ge(gelu_done, KF * s + (k + 1))
                    pe.matmul(ps_w[:, 0:D], hidT[:, k, :], experts[:, bass.ds(e * EW + (C * FF + k * D), D)],
                              start=False, stop=(k == KF - 1)).then_inc(y_part, 1)

            pe.wait_ge(tables, 2)
            rows_transposed(16)
            hidden(0)
            rows_transposed(32)

            def steady(s):
                hidden(s + 1)
                rows_transposed(16 * s + 48)
                result(s)

            pe.wait_ge(ld_early, 32 * EARLY)
            with pe.Fori(0, EARLY) as s:
                steady(s)
            pe.wait_ge(ld_late, 32 * (X - 1 - EARLY))
            with pe.Fori(EARLY, X - 1) as s:
                steady(s)
            pe.wait_ge(ld_last, 32)
            with pe.Fori(X - 1, SLOTS - 2) as s:
                steady(s)
            hidden(SLOTS - 1)
            result(SLOTS - 2)
            result(SLOTS - 1)

        @block.vector
        def _(dve):
            done = [0]

            def step(ins):
                done[0] += 1
                ins.then_inc(pre_step, 1)
                dve.wait_ge(pre_step, done[0])

            dve.memset(vbd[:, :, :], 0.0).then_inc(pre_step, 1)
            dve.memset(count[:, :], 0.0).then_inc(pre_step, 1)
            done[0] += 2
            dve.wait_ge(ld_vecs, 16)
            dve.tensor_copy(vpart[:, 0, :], vecs[:, :]).then_inc(split_ready, 1)
            dve.wait_ge(split_ready, 1)
            step(dve.tensor_tensor(vres[:, 0, :], vecs[:, :], vpart[:, 0, :], ALU.subtract))
            dve.tensor_copy(vpart[:, 1, :], vres[:, 0, :]).then_inc(split_ready, 1)
            dve.wait_ge(split_ready, 2)
            step(dve.tensor_tensor(vres[:, 1, :], vres[:, 0, :], vpart[:, 1, :], ALU.subtract))
            dve.tensor_copy(vpart[:, 2, :], vres[:, 1, :]).then_inc(split_ready, 1)

            def statistics_of(i):
                dve.wait_ge(ld_x[i], 16)
                for t in range(i * TILES, (i + 1) * TILES):
                    tile_statistics(t)
                aggregate(i)

            def tile_statistics(t):
                dve.bn_stats(fstat0[:, t, :], x[:, t, :]).then_inc(pre_step, 1)
                done[0] += 1

            def aggregate(i):
                dve.wait_ge(pre_step, done[0])
                for t in range(i * TILES, (i + 1) * TILES):
                    dve.bn_aggr(mv0[:, t, :], fstat0[:, t, :]).then_inc(mv0_ready, 1)

            statistics_of(0)
            dve.wait_ge(ld_small, 32)
            step(dve.tensor_scalar(omu[:, :], cols[:, MU_R:MU_R + 4], -1.0, 1.0, ALU.mult, ALU.add))
            step(dve.tensor_scalar(tau[:, :], tau[:, :], 1.0 / E ** 0.5, None, ALU.mult))
            n = 0
            for l in range(2):
                for c in range(C):
                    dve.wait_ge(pre_mm, n + 1)
                    for b in range(B):
                        dve.tensor_scalar(keys[:, l * C + c, b * S:(b + 1) * S], (ps_w, ps_o)[n % 2][:, b * S:(b + 1) * S],
                                          cols[:, BK[l] + c:BK[l] + c + 1], tau[:, b:b + 1], ALU.add, ALU.mult).then_inc(pre_ev, 1)
                    n += 1
            assert NT == TILES + 2 * B
            dve.wait_ge(ld_x[1], 16)
            for l in range(2):
                for b in range(B):
                    dve.wait_ge(pre_mm, n + 1)
                    for q in range(2):
                        half = slice(q * S, (q + 1) * S)
                        at = (l * B + b) * PAIRS
                        to = vbd[half, at:at + PAIRS, q * (E + 1):q * (E + 1) + E]
                        frm = (ps_w, ps_o)[n % 2][half, 0:D].rearrange("s (a q d) -> s a q d", q=2, d=E)[:, :, q, :]
                        dve.tensor_copy(to, frm).then_inc(pre_ev, 1)
                    n += 1
                    tile_statistics(TILES + l * B + b)
            aggregate(1)
            for q in range(2):
                col = q * (E + 1) + E
                step(dve.memset(vbd[q * S:(q + 1) * S, :, col:col + 1], 1.0))
            dve.wait_ge(const_ready, 11)
            dve.wait_ge(rstd0_ready, B // PAIR)

            links = [0]

            def mark(ins):
                links[0] += 1
                ins.then_inc(dve_step.sem, 1)
                return links[0]

            def link(b, ins):
                n = mark(ins)
                dve.wait_ge(dve_step.sem, dve_step.value(b, n))

            with dve.Fori(0, B // PAIR) as i:
                links[0] = 0

                def tile_of(t):
                    return x[:, bass.ds(i * TILES + t, 1), :].rearrange("p t d -> p (t d)")

                def statistics(t):
                    dve.sem_inc(passed, 1)
                    link(i, dve.bn_stats(fstat[:, t, :], tile_of(t)))
                    dve.sem_inc(passed, 1)
                    dve.bn_aggr(mv[:, t, :], fstat[:, t, :]).then_inc(mv_ready.sem, 1)

                def norm(k, g, j):
                    t = g * JT + j
                    if k == 0:
                        dve.wait_ge(rows_free[g], i + 1)
                        mean, scale = mv0[:, bass.ds(i * TILES + t, 1), 0], rstd0[:, bass.ds(i * TILES + t, 1)]
                    else:
                        n = (k - 1) * TILES + t + 1
                        dve.wait_ge(mv_ready.sem, mv_ready.value(i, n))
                        dve.wait_ge(rstd_ready.sem, rstd_ready.value(i, n))
                        mean, scale = mv[:, t, 0:1], rstd[:, t:t + 1]
                    dve.tensor_scalar(xn[:, t, 0:D], tile_of(t), mean, scale, ALU.subtract, ALU.mult).then_inc(xn_ready.sem, 1)

                def shift(n):
                    for c in range(C):
                        dve.wait_ge(s_done.sem, s_done.value(i, n * C + c + 1))
                        scores = ps_s[:, c * 512:(c + 1) * 512].rearrange("p (h s) -> p h s", h=G)
                        top = smax[:, c * G:(c + 1) * G]
                        link(i, dve.tensor_reduce(top, scores, AX_X, ALU.max))
                        if n:
                            dve.wait_ge(exp_done.sem, exp_done.value(i, (n - 1) * C + c + 1))
                        dve.tensor_tensor(shifted[:, c * 512:(c + 1) * 512].rearrange("p (h s) -> p h s", h=G), scores,
                                          top.unsqueeze(2).to_broadcast([P, G, S]), ALU.subtract).then_inc(sub_done.sem, 1)

                def values(n):
                    dve.wait_ge(pv_done.sem, pv_done.value(i, n + 1))
                    sums = ps_o[:, 0:PAIRS * VW].rearrange("p (h w) -> p h w", h=H)
                    link(i, dve.reciprocal(rsum[:, :], sums[:, :, E]))
                    dve.tensor_tensor(onorm[:, :].rearrange("p (h e) -> p h e", h=H), sums[:, :, 0:E],
                                      rsum[:, :].unsqueeze(2).to_broadcast([P, H, E]), ALU.mult).then_inc(on_done.sem, 1)

                def project(n):
                    t = n % ATT
                    dve.wait_ge(pr_done.sem, pr_done.value(i, n + 1))
                    dve.tensor_tensor(tile_of(t), tile_of(t), ps_w[:, 0:D], ALU.add).then_inc(x_done.sem, 1)
                    dve.wait_ge(x_done.sem, x_done.value(i, ADDED["project", n]))
                    statistics(t)

                def mix(g, w):
                    for c in range(C):
                        dve.wait_ge(prev_done.sem, prev_done.value(i, (g * 2 + w) * C + c + 1))
                        mu = (MU_K, MU_R)[w] + c
                        dve.scalar_tensor_tensor(out=mixed(w, g, c), in0=xnT[:, g, c, 1:L + 1], scalar=cols[:, mu:mu + 1],
                                                 in1=mixed(w, g, c), op0=ALU.mult, op1=ALU.add).then_inc(
                                                     (mixk_done, mixr_done)[w].sem, 1)

                def square(g):
                    for c in range(C):
                        dve.wait_ge(relu_done.sem, relu_done.value(i, g * C + c + 1))
                        dve.tensor_tensor(kact(g, c), kact(g, c), kact(g, c), ALU.mult).then_inc(kact_done.sem, 1)

                def value(g, h):
                    dve.wait_ge(gate_done.sem, gate_done.value(i, g * 2 + h + 1))
                    tiles = [g * JT + 2 * h + m for m in range(2)]
                    for m, t in enumerate(tiles):
                        dve.wait_ge(val_done.sem, val_done.value(i, t + 1))
                        dve.scalar_tensor_tensor(out=gated[m], in0=gate_of(g, h)[:, m * D:(m + 1) * D], scalar=1.0,
                                                 in1=(ps_w, ps_o)[m][:, 0:D], op0=ALU.add, op1=ALU.mult).then_inc(gated_done.sem, 1)
                    for m, t in enumerate(tiles):
                        dve.wait_ge(gated_done.sem, gated_done.value(i, t + 1))
                        dve.scalar_tensor_tensor(out=tile_of(t), in0=gated[m], scalar=0.5, in1=tile_of(t),
                                                 op0=ALU.mult, op1=ALU.add).then_inc(x_done.sem, 1)
                    for m, t in enumerate(tiles):
                        dve.wait_ge(x_done.sem, x_done.value(i, ADDED["value", g, h] + (m - 1)))
                        dve.sem_inc(passed, 1)
                        n = mark(dve.bn_stats(fstat[:, t, :], tile_of(t)))
                    for m, t in enumerate(tiles):
                        dve.wait_ge(dve_step.sem, dve_step.value(i, n + (m - 1)))
                        dve.sem_inc(passed, 1)
                        dve.bn_aggr(mv[:, t, :], fstat[:, t, :]).then_inc(mv_ready.sem, 1)

                def spread(a):
                    return a.unsqueeze(2).to_broadcast([P, JT, X])

                def along(a):
                    return a.unsqueeze(1).to_broadcast([P, JT, X])

                def pick(g, p, top, first, hot, t1, t2):
                    link(i, dve.tensor_reduce(r1[:, g, top], r8[:, g, p], AX_X, ALU.max))
                    link(i, dve.tensor_tensor(r8[:, g, t1], r8[:, g, p], spread(r1[:, g, top]), ALU.is_equal))
                    link(i, dve.scalar_tensor_tensor(out=r8[:, g, t2], in0=r8[:, g, t1], scalar=float(-X),
                                                     in1=along(iota8[:, :]), op0=ALU.mult, op1=ALU.add))
                    link(i, dve.tensor_reduce(r1[:, g, first], r8[:, g, t2], AX_X, ALU.min))
                    link(i, dve.tensor_tensor(r8[:, g, hot], along(iota8m[:, :]), spread(r1[:, g, first]), ALU.is_equal))

                def choose(g, part):
                    mine = slice(g * JT, (g + 1) * JT)
                    if part == 0:
                        dve.wait_ge(turn_read.sem, turn_read.value(i, TURN["logits", g] + 1))
                        link(i, dve.tensor_reduce(r1[:, g, 0], r8[:, g, 10], AX_X, ALU.max))
                        dve.tensor_tensor(r8[:, g, 0], r8[:, g, 10], spread(r1[:, g, 0]), ALU.subtract).then_inc(lsub_done.sem, 1)
                    elif part == 1:
                        dve.wait_ge(lexp_done.sem, lexp_done.value(i, g + 1))
                        link(i, dve.tensor_reduce(r1[:, g, 1], r8[:, g, 1], AX_X, ALU.add))
                        link(i, dve.reciprocal(r1[:, g, 2], r1[:, g, 1]))
                        link(i, dve.tensor_tensor(r8[:, g, 2], r8[:, g, 1], spread(r1[:, g, 2]), ALU.mult))
                        pick(g, 2, 3, 4, 3, 4, 5)
                        link(i, dve.scalar_tensor_tensor(out=r8[:, g, 6], in0=r8[:, g, 3], scalar=-2.0, in1=r8[:, g, 2],
                                                         op0=ALU.mult, op1=ALU.add))
                    elif part == 2:
                        pick(g, 6, 5, 8, 7, 4, 5)
                        dve.tensor_tensor(chosen[:, mine, :], r8[:, g, 3], r8[:, g, 7], ALU.add).then_inc(chosen_done.sem, 1)
                        dve.tensor_tensor(r1[:, g, 6], r1[:, g, 5], r1[:, g, 3], ALU.subtract).then_inc(gap_done.sem, 1)
                    else:
                        mark(dve.tensor_scalar(xn[:, mine, FIRST], r1[:, g, 4], float(X), None, ALU.add))
                        mark(dve.tensor_copy(xn[:, mine, TOKEN], token[:, bass.ds(i * TILES + g * JT, JT)]))
                        dve.wait_ge(gexp_done.sem, gexp_done.value(i, g + 1))
                        link(i, dve.tensor_scalar(r1[:, g, 8], r1[:, g, 7], 1.0, None, ALU.add))
                        link(i, dve.reciprocal(r1[:, g, 9], r1[:, g, 8]))
                        mark(dve.tensor_copy(xn[:, mine, W1ST], r1[:, g, 9]))
                        mark(dve.tensor_tensor(xn[:, mine, W2ND], r1[:, g, 9], r1[:, g, 7], ALU.mult))

                def places(g):
                    dve.wait_ge(turn_read.sem, turn_read.value(i, TURN["ranks", g] + 1))
                    for t in range(JT):
                        mark(dve.tensor_tensor(r8[:, g, 8, t], ranks[:, g, 0, t], count[:, :], ALU.add))
                        link(i, dve.tensor_tensor(count[:, :], ranks[:, g, 1, t], count[:, :], ALU.add))
                    link(i, dve.tensor_tensor(r8[:, g, 9], r8[:, g, 8], along(region[:, :]), ALU.add))
                    for k in range(2):
                        link(i, dve.tensor_tensor(r8[:, g, 4 + k], r8[:, g, 9], r8[:, g, 3 + 4 * k], ALU.mult))
                        link(i, dve.tensor_reduce(r1[:, g, 3 + k], r8[:, g, 4 + k], AX_X, ALU.add))
                        link(i, dve.tensor_copy(where_[:, k, g * JT:(g + 1) * JT], r1[:, g, 3 + k]))
                    dve.sem_inc(packed_done.sem, 1)

                stage_of({"norm": norm, "shift": shift, "values": values, "project": project,
                          "mix": mix, "square": square, "value": value, "choose": choose, "places": places})
                assert links[0] == DVE_STEPS, links[0]

            done[0] = 0

            def tstep(ins):
                done[0] += 1
                ins.then_inc(tab_step, 1)
                dve.wait_ge(tab_step, done[0])

            def over_slots(a):
                return a.unsqueeze(1).to_broadcast([P, SLOTS, X])

            tstep(dve.tensor_scalar(tt[:, 0, :], count[:, :], float(P - 1), None, ALU.add))
            tstep(dve.tensor_copy(tti[:, :], tt[:, 0, :]))
            tstep(dve.tensor_scalar(tti[:, :], tti[:, :], 7, None, ALU.logical_shift_right))
            tstep(dve.tensor_copy(tt[:, 1, :], tti[:, :]))
            tstep(dve.tensor_scalar(tt[:, 1, :], tt[:, 1, :], 1.0, None, ALU.max))
            tstep(dve.memset(tt[:, 2, :], 1.0))
            tstep(dve.tensor_tensor_scan(tt[:, 3, :], tt[:, 2, :], tt[:, 1, :], 0.0, ALU.mult, ALU.add))
            tstep(dve.tensor_tensor(ge, iota_s[:, :].unsqueeze(2).to_broadcast([P, SLOTS, X]),
                                    over_slots(tt[:, 3, :]), ALU.is_ge))
            tstep(dve.tensor_reduce(st[:, 0, :], ge, AX_X, ALU.add))
            tstep(dve.tensor_tensor(gen, ge, over_slots(tt[:, 1, :]), ALU.mult))
            tstep(dve.tensor_reduce(st[:, 1, :], gen, AX_X, ALU.add))
            tstep(dve.tensor_tensor(st[:, 2, :], iota_s[:, :], st[:, 1, :], ALU.subtract))
            tstep(dve.scalar_tensor_tensor(out=st[:, 3, :], in0=st[:, 0, :], scalar=float(REGION // P), in1=st[:, 2, :],
                                           op0=ALU.mult, op1=ALU.add))
            tstep(dve.tensor_scalar(st[:, 4, :], st[:, 0, :], float(X - 1), None, ALU.min))
            dve.tensor_scalar(slot_row[:, :], st[0:1, 3, :], float(P), None, ALU.mult).then_inc(tables, 1)
            dve.tensor_copy(slot_exp[:, :], st[0:1, 4, :]).then_inc(tables, 1)
            dve.sem_inc(ps_y_free, 1)
            dve.sem_inc(ysb_free, 1)

            def column(a, s, k):
                return a[:, bass.ds(s, 1), k:k + 1].rearrange("p s w -> p (s w)")

            def take(s, n_loaded):
                dve.wait_ge(xg_loaded, n_loaded)
                dve.tensor_copy(slot_cols[:, bass.ds(s, 1), :].rearrange("p s w -> p (s w)"),
                                xg[:, D:RW]).then_inc(wi_out, 1)

            def copy_first_matrix(s):
                e = dve.value_load(slot_exp[0:1, bass.ds(s, 1)], min_val=0, max_val=X - 1)
                for q in range(QUARTERS):
                    if not (isinstance(s, int) and s == 0):
                        dve.wait_ge(hid_done, QUARTERS * s + (q + 1 - QUARTERS))
                    at = q * QK * P
                    frm = experts[:, bass.ds(e * EW, C * FF)].rearrange("p (c f) -> p c f", c=C)
                    dve.tensor_copy(w1s[:, :, at:at + QK * P], frm[:, :, at:at + QK * P]).then_inc(w1_ready, 1)

            TABS = done[0]
            SLOT_STEPS = 4

            def weigh(s):
                dve.wait_ge(wi_out, s + 1)
                expert = st[:, 4, bass.ds(s, 1)]
                for k, (col, test) in enumerate([(0, ALU.is_equal), (1, ALU.not_equal)]):
                    dve.tensor_scalar(column(slot_w, s, k), column(slot_cols, s, FIRST - D), expert,
                                      column(slot_cols, s, col), test, ALU.mult).then_inc(tab_step, 1)
                dve.wait_ge(tab_step, SLOT_STEPS * s + (TABS + 2))
                dve.tensor_tensor(column(slot_w, s, 2), column(slot_w, s, 0), column(slot_w, s, 1), ALU.add).then_inc(tab_step, 1)
                dve.wait_ge(ysb_free, s + 1)
                dve.tensor_copy(slot_tok[:, :], column(slot_cols, s, TOKEN - D)).then_inc(tab_step, 1)
                dve.wait_ge(tab_step, SLOT_STEPS * s + (TABS + 4))
                dve.wait_ge(y_part, KF * s + KF)
                dve.tensor_scalar(ysb[:, :], ps_w[:, 0:D], column(slot_w, s, 2), None, ALU.mult).then_inc(ps_y_free, 1)
                dve.wait_ge(ps_y_free, s + 2)
                dve.sem_inc(tok_out, 1)

            dve.wait_ge(tables, 2)
            dve.wait_ge(xout, 16 * (B // PAIR + 1))
            dve.wait_ge(ld_early, 32 * EARLY)
            copy_first_matrix(0)
            take(0, 16)
            take(1, 32)
            copy_first_matrix(1)

            def steady(s):
                take(s + 2, 16 * s + 48)
                copy_first_matrix(s + 2)
                weigh(s)

            with dve.Fori(0, EARLY - 2) as s:
                steady(s)
            dve.wait_ge(ld_late, 32 * (X - 1 - EARLY))
            with dve.Fori(EARLY - 2, X - 3) as s:
                steady(s)
            dve.wait_ge(ld_last, 32)
            with dve.Fori(X - 3, SLOTS - 2) as s:
                steady(s)
            weigh(SLOTS - 2)
            weigh(SLOTS - 1)


def kernel(**inputs):
    import numpy as np
    import concourse.bacc as bacc
    from concourse.bass_utils import run_bass_kernel_spmd

    def get(name):
        return np.ascontiguousarray(inputs[name])

    ctx = get("ctx_1024").transpose(2, 0, 1)
    ctx = np.ascontiguousarray(np.concatenate([ctx, ctx], axis=2)).reshape(D, B * 2 * S)
    names = ["L0_xcond_Wk", "L1_xcond_Wk", "L0_xcond_Wv", "L1_xcond_Wv", "L0_xcond_Wq", "L1_xcond_Wq", "L0_xcond_Wo",
             "L1_xcond_Wo", "L0_ffn_W_r", "L0_ffn_W_k", "L0_ffn_W_v"]
    mats = np.ascontiguousarray(np.stack([get(n).T for n in names]))
    by_col = ["L0_xcond_bq", "L0_xcond_bk", "L1_xcond_bq", "L1_xcond_bk", "L0_ffn_mu_r", "L0_ffn_mu_k", "L1_ffn_b1"]
    cols = np.ascontiguousarray(np.concatenate([get(n).reshape(-1, P) for n in by_col]).T)
    by_row = ["fside_BxS2_0", "L0_xcond_bo", "L1_xcond_bo", "L0_xcond_bv", "L1_xcond_bv", "L1_ffn_b2", "L1_ffn_br"]
    vecs = np.concatenate([get(n).reshape(-1) for n in by_row])
    vecs = np.concatenate([vecs, np.zeros(VECS - vecs.size, vecs.dtype)])
    arrays = {
        "in_x": get("x").reshape(B * L, D), "in_ctx": ctx, "in_tau": get("condB_tau"), "in_mats": mats, "in_cols": cols,
        "in_vecs": vecs, "in_w1": get("L1_ffn_W1"), "in_w2": get("L1_ffn_W2"), "in_wr": get("L1_ffn_Wr"),
    }
    nc = bacc.Bacc("TRN2", target_bir_lowering=False, num_devices=1)
    args = [nc.dram_tensor(n, a.shape, mybir.dt.from_np(a.dtype), kind="ExternalInput").ap() for n, a in arrays.items()]
    args.append(nc.dram_tensor("out_x", (B * L + P, D), F32, kind="ExternalOutput").ap())
    build(nc, *args)
    r = run_bass_kernel_spmd(nc, [arrays], core_ids=[0])
    return r.results[0]["out_x"][0:B * L].reshape(B, L, D)
```

```python
from contextlib import ExitStack

import concourse.bass as bass
from concourse import mybir

F32, BF16 = mybir.dt.float32, mybir.dt.bfloat16
I32, U32 = mybir.dt.int32, mybir.dt.uint32
ALU = mybir.AluOpType
ACT = mybir.ActivationFunctionType
AX_X = mybir.AxisListType.X

P = 128
B, L, S, D = 4, 512, 64, 256
H, E = 16, 16
C = D // P
JT = L // P
NT = B * JT
G = H // C
PAIRS = H // 2
VW = 2 * (E + 1)
X, FF = 8, 1024
KF = FF // P
EPS = 1e-5

REGION = B * L
SLOTS = (2 * B * L - X) // P + X
SPARE = SLOTS - 2 * B * L // P
ROWS = X * REGION + SPARE * P
RW = D + 4
W1ST, W2ND, FIRST, TOKEN = range(D, RW)

PAIR = 2
TILES = PAIR * JT
HALVES = JT // 2
ATT = PAIR * JT

WK, WV, WQ, WO = (0, 1), (2, 3), (4, 5), (6, 7)
FR, FK, FV = 8, 9, 10
MATS = 11
MATS_LOADED = (0, 2, 5, MATS)

DELTA = 0
BO = (B * S, B * S + D)
BV = (BO[1] + D, BO[1] + 2 * D)
B2 = BV[1] + D
BR = B2 + X * D
VECW = -(-(BR + X) // P)
VECS = VECW * P
BQ, BK, MU_R, MU_K = (0, 4), (2, 6), 8, 10
B1 = 12
TAU = B1 + X * KF
COLS = TAU + B


def order_of_stages():
    out = []

    def turns(k, g):
        return [(stage, k, g, h) for h in range(HALVES) for stage in ("turn", "turned")]

    def norms(k, g, tiles=range(JT)):
        return [("norm", k, g, j) for j in tiles]

    def attention(l, start, between):
        first, last = l * ATT, (l + 1) * ATT - 1
        out.extend([("scores", first), ("shift", first), ("exp", first)] + start)
        for n in range(first, last + 1):
            out.append(("turn_probs", n))
            if n > first + 1:
                out.append(("norm", 2 * l + 1, (n - 2 - first) // JT, (n - 2 - first) % JT))
            if n > first:
                out.append(("turn_out", n - 1))
            if n < last:
                out.extend([("scores", n + 1), ("shift", n + 1)])
                out.extend(between.get("exp", []) if n == first else [])
                out.append(("exp", n + 1))
            else:
                out.extend(between.get(-1, []))
            out.append(("values", n))
            if n > first:
                out.append(("project", n - 1))
            out.extend(between.get(n - first, []))
        out.append(("turn_out", last))
        out.append(("norm", 2 * l + 1, PAIR - 1, JT - 2))
        out.extend(between.get(ATT, []) + [("project", last), ("norm", 2 * l + 1, PAIR - 1, JT - 1)])

    out.extend(norms(0, 0) + turns(0, 0) + [("queries", 0, 0), ("keys", 0, 0), ("keys", 0, 1)] + norms(0, 1) + turns(0, 1))
    attention(0, [("queries", 0, 1)],
              {JT: turns(1, 0)[:2], JT + 1: turns(1, 0)[2:] + [("before", 0, 0), ("mix", 0, 0)], JT + 2: [("before", 0, 1), ("mix", 0, 1)],
               -1: [("key", 0)], ATT: [("gate", 0)]})
    out.extend([("value", 0, 0), ("add", 0, 0)] + turns(1, 1) + [("before", 1, 0), ("before", 1, 1), ("mix", 1, 0)])
    out.extend([("value", 0, 1), ("add", 0, 1), ("key", 1)] + norms(2, 0, (0, 1)) + [("mix", 1, 1)] + norms(2, 0, (2, 3)) + turns(2, 0))
    out.extend([("keys", 1, 0), ("gate", 1), ("queries", 1, 0), ("value", 1, 0), ("add", 1, 0)])
    attention(1, [("value", 1, 1)] + norms(2, 1, (0, 1)) + [("add", 1, 1)] + norms(2, 1, (2, 3)),
              {"exp": turns(2, 1)[1::2], 0: [("keys", 1, 1)] + turns(2, 1)[::2] + [("queries", 1, 1)],
               JT: turns(3, 0)[:2], JT + 1: turns(3, 0)[2:] + [("logits", 0, 0), ("logits", 0, 1), ("choose", 0, 0), ("choose", 0, 1)],
               JT + 2: [("choose", 0, 2)], JT + 3: [("ranks", 0)]})
    out.extend(turns(3, 1)[:2] + [("choose", 0, 3), ("places", 0), ("logits", 1, 0)] + turns(3, 1)[2:] + [("logits", 1, 1)])
    out.extend(("scatter", 0, j) for j in range(JT))
    out.extend([("choose", 1, part) for part in range(4)] + [("ranks", 1), ("places", 1)])
    out.extend(("scatter", 1, j) for j in range(JT))
    return out


ORDER = order_of_stages()
TURN = {s: n for n, s in enumerate(x for x in ORDER if x[0] in ("turn", "turn_out", "logits", "ranks"))}
ADDED = {}
for s in ORDER:
    if s[0] in ("project", "add"):
        ADDED[s] = max(ADDED.values(), default=0) + {"project": 1, "add": 2}[s[0]]


VALUE_BANKS = ("ow", "wo")


class Signal:

    def __init__(self, sem, per):
        self.sem, self.per = sem, per

    def value(self, i, k):
        return i * self.per + k


def build(nc, x_in, ctx_in, mats_in, cols_in, vecs_in, w1_in, w2_in, wr_in, out):
    routed = nc.dram_tensor("routed_rows", (ROWS, RW), F32, kind="Internal").ap()
    stack = ExitStack()
    with stack:
        def sb(name, shape, dt=F32):
            return stack.enter_context(nc.sbuf_tensor(name, shape, dt))

        def pb(name, width):
            return stack.enter_context(nc.psum_tensor(name, [P, width], F32))

        def sem(name):
            return stack.enter_context(nc.semaphore(name))

        def signal(name, per):
            return Signal(sem(name), per)

        EW = C * FF + KF * D
        EARLY = 4
        experts = sb("experts", [P, X * EW])
        room = [EARLY * EW]

        def lent(*dims):
            n = 1
            for d in dims:
                n *= d
            a = experts[:, room[0]:room[0] + n]
            room[0] += n
            assert room[0] <= X * EW
            names = "abcd"[:len(dims)]
            if len(dims) > 1:
                kw = {names[i]: dims[i] for i in range(1, len(dims))}
                a = a.rearrange(f"p ({' '.join(names)}) -> p {' '.join(names)}", **kw)
            return a

        vbd = lent(2 * B * PAIRS, VW)
        keys = lent(2 * C, B * S)
        mats = lent(MATS * C, D)
        kbd = lent(PAIR, C, G * S)
        shifted = lent(L * C)
        assert room[0] <= (X - 1) * EW
        qT = lent(PAIR, C, L)
        xnT = lent(PAIR, C, L + 1)

        def mat(m, c):
            return mats[:, m * C + c, :]

        x = sb("x", [P, NT, D])
        rows3 = sb("rows3", [3, VECS], BF16)
        xn = sb("xn", [P, TILES, RW])
        probs = sb("probs", [P, H * S])
        probsT = sb("probsT", [P, PAIRS, P])
        onorm = sb("onorm", [P, D])
        oT = sb("oT", [P, 2, C, P])
        gated = [oT[:, m, :, :].rearrange("p c t -> p (c t)") for m in range(2)]
        ident = sb("ident", [P, P])
        tri = sb("tri", [P, P], BF16)
        ones = sb("ones", [P, P], BF16)
        ones3 = ones[0:3, :]
        quarter = sb("quarter", [3, P], BF16)
        mask = sb("mask", [P, G])
        cols = sb("cols", [P, COLS])
        omu = sb("omu", [P, 4])
        wr = sb("wr", [P, C, X])
        tau = sb("tau", [P, B])
        halfneg = sb("halfneg", [P, 1])
        fstat = sb("fstat", [P, TILES, 6])
        mv = sb("mv", [P, TILES, 2])
        veps = sb("veps", [P, TILES])
        rstd = sb("rstd", [P, TILES])
        fstat0 = sb("fstat0", [P, NT, 6])
        mv0 = sb("mv0", [P, NT, 2])
        rstd0 = sb("rstd0", [P, NT])
        smax = sb("smax", [P, H])
        rsum = sb("rsum", [P, H])
        r8 = sb("r8", [P, PAIR, 11, JT, X])
        r1 = sb("r1", [P, PAIR, 10, JT])
        ranks = sb("ranks", [P, PAIR, 2, JT, X])
        chosen = sb("chosen", [P, TILES, X], BF16)
        iota8 = sb("iota8", [P, X])
        iota8m = sb("iota8m", [P, X])
        region = sb("region", [P, X])
        token = sb("token", [P, NT])
        count = sb("count", [P, X])
        where_ = sb("where", [P, 2, TILES], U32)
        vecs = sb("vecs", [P, VECW])
        vres = sb("vres", [P, 2, VECW])
        vpart = sb("vpart", [P, 3, VECW], BF16)
        ctxT = probs[:, :].rearrange("p (c b s) -> p c b s", c=C, b=B)

        QUARTERS = 4
        QK = KF // QUARTERS

        def hidden_chunk(k):
            q, at = k // QK, k % QK * P
            return (ps_s, ps_p)[q // 2][:, q % 2 * 512 + at:q % 2 * 512 + at + P]

        xg = xn[:, 0, :]
        xgT = oT[:, 0, :, :]
        hidT = probsT
        w1s = x[:, 0:C * FF // D, :].rearrange("p t d -> p (t d)").rearrange("p (c f) -> p c f", c=C)
        ysb = onorm
        empty = sb("empty", [P, RW])
        slot_cols = sb("slot_cols", [P, SLOTS, RW - D])
        slot_w = sb("slot_w", [P, SLOTS, 3])
        slot_tok = sb("slot_tok", [P, 1], U32)
        iota_s = sb("iota_s", [P, SLOTS])
        ge = probs[:, 0:SLOTS * X].rearrange("p (s e) -> p s e", e=X)
        gen = probs[:, SLOTS * X:2 * SLOTS * X].rearrange("p (s e) -> p s e", e=X)
        tt = sb("tt", [P, 4, X])
        tti = sb("tti", [P, X], I32)
        st = sb("st", [P, 5, SLOTS])
        slot_row = sb("slot_row", [1, SLOTS], I32)
        slot_exp = sb("slot_exp", [1, SLOTS], I32)

        ps_t = [pb("ps_t0", 512), pb("ps_t1", 512)]
        ps_s = pb("ps_s", 1024)
        ps_p = pb("ps_p", 1024)
        ps_o = pb("ps_o", 512)
        ps_w = pb("ps_w", 512)
        bank_of = {"o": ps_o, "w": ps_w}
        pre_banks = [ps_w, ps_o] + ps_t

        ld_ctx, *ld_mats, ld_small, ld_vecs = (sem(n) for n in ("ld_ctx", "ld_mats0", "ld_mats1", "ld_mats2", "ld_small", "ld_vecs"))
        ld_wr = sem("ld_wr")
        ld_x = [sem(f"ld_x{i}") for i in range(B // PAIR)]
        ld_rows3, ld_fill, ld_experts = (sem(n) for n in ("ld_rows3", "ld_fill", "ld_experts"))
        experts_ready = sem("experts_ready")
        mv0_ready, rstd0_ready = sem("mv0_ready"), sem("rstd0_ready")
        const_ready = sem("const_ready")
        const_step = sem("const_step")
        split_ready = sem("split_ready")
        pre_step = sem("pre_step")
        pre_mm = sem("pre_mm")
        keys_out = sem("keys_out")
        vals_out = sem("vals_out")

        DVE_STEPS = 136
        dve_step = signal("dve_step", DVE_STEPS)
        pool_step = signal("pool_step", 24)
        mv_ready = signal("mv_ready", 24)
        rstd_ready = signal("rstd_ready", 24)
        xn_ready = signal("xn_ready", 32)
        turned = signal("turned", len(TURN))
        turn_read = signal("turn_read", len(TURN))
        q_done = signal("q_done", 2 * PAIR * C)
        q_out = signal("q_out", 2 * PAIR * C)
        kbd_ready = signal("kbd_ready", 2 * PAIR * C)
        s_done = signal("s_done", 2 * ATT * C)
        sub_done = signal("sub_done", 2 * ATT * C)
        exp_done = signal("exp_done", 2 * ATT * C)
        pt_done = signal("pt_done", 2 * ATT * C)
        pt_out = signal("pt_out", 2 * ATT * C)
        pv_done = signal("pv_done", 2 * ATT)
        on_done = signal("on_done", 2 * ATT)
        pr_done = signal("pr_done", 2 * ATT)
        x_done = signal("x_done", max(ADDED.values()))
        prev_done = signal("prev_done", PAIR * 2 * C)
        mixk_done = signal("mixk_done", PAIR * C)
        mixr_done = signal("mixr_done", PAIR * C)
        key_done = signal("key_done", PAIR * C)
        relu_done = signal("relu_done", PAIR * C)
        kact_done = signal("kact_done", PAIR * C)
        rg_done = signal("rg_done", PAIR * 2)
        gate_done = signal("gate_done", PAIR * 2)
        val_done = signal("val_done", PAIR * JT)
        gated_done = signal("gated_done", PAIR * JT)
        lsub_done = signal("lsub_done", PAIR)
        lexp_done = signal("lexp_done", PAIR)
        gap_done = signal("gap_done", PAIR)
        gexp_done = signal("gexp_done", PAIR)
        chosen_done = signal("chosen_done", PAIR)
        packed_done = signal("packed_done", PAIR)
        rows_free = [sem(f"rows_free{g}") for g in range(PAIR)]
        scattered = [signal(f"scattered{g}", 16 * 2 * JT) for g in range(PAIR)]
        passed = sem("passed")
        xout = sem("xout")

        tab_step = sem("tab_step")
        tables = sem("tables")
        xg_loaded = sem("xg_loaded")
        wi_out = sem("wi_out")
        xt_done = sem("xt_done")
        xt_out = sem("xt_out")
        w1_ready = sem("w1_ready")
        hid_done = sem("hid_done")
        gelu_done = sem("gelu_done")
        y_part = sem("y_part")
        ps_y_free = sem("ps_y_free")
        tok_out = sem("tok_out")
        ysb_free = sem("ysb_free")
        added = sem("added")

        PRE_KEYS = 2 * C
        PRE_VALS = 2 * B

        def mixed(w, g, c):
            return (qT, kbd)[w][:, g, c, :]

        def kact(g, c):
            return xnT[:, g, c, 1:L + 1]

        def gate_of(g, half):
            return qT[:, g, half, :]

        def stage_of(own):
            for stage, *which in ORDER:
                if stage in own:
                    own[stage](*which)

        def load_expert(eng, e):
            at = e * EW
            eng.dma_start(experts[:, at:at + C * FF].rearrange("p (c f) -> p c f", c=C),
                          w1_in[e].rearrange("(c p) f -> p c f", p=P)).then_inc(ld_experts, 16)
            eng.dma_start(experts[:, at + C * FF:at + EW].rearrange("p (k d) -> p k d", k=KF),
                          w2_in[e].rearrange("(k p) d -> p k d", p=P)).then_inc(ld_experts, 16)

        block = stack.enter_context(nc.Block())

        @block.sync
        def _(sp):
            sp.dma_start(ctxT, ctx_in.rearrange("(c p) (b s) -> p c b s", p=P, b=B)).then_inc(ld_ctx, 16)
            src = mats_in.rearrange("m (c p) n -> p (m c) n", p=P)
            x_tiles = x_in.rearrange("(t p) d -> p t d", p=P)

            def load_mats(k):
                part = slice(MATS_LOADED[k] * C, MATS_LOADED[k + 1] * C)
                sp.dma_start(mats[:, part, :], src[:, part, :]).then_inc(ld_mats[k], 16)

            load_mats(0)
            sp.dma_start(x[:, 0:TILES, :], x_tiles[:, 0:TILES, :]).then_inc(ld_x[0], 16)
            sp.wait_ge(split_ready, 3)
            for i in range(3):
                sp.dma_start(rows3[i:i + 1, :].rearrange("o (p k) -> o p k", k=VECW), vpart[:, i, :]).then_inc(ld_rows3, 16)
            load_mats(1)
            sp.dma_start(x[:, TILES:NT, :], x_tiles[:, TILES:NT, :]).then_inc(ld_x[1], 16)
            load_mats(2)
            sp.wait_ge(const_ready, 1)
            sp.dma_start(routed.rearrange("(n p) k -> p n k", p=P),
                         empty[:, :].unsqueeze(1).to_broadcast([P, ROWS // P, RW])).then_inc(ld_fill, 16)
            for e in range(EARLY):
                load_expert(sp, e)
            sp.wait_ge(ld_experts, 32 * EARLY)
            sp.sem_inc(experts_ready, EARLY)

            def write_out(i):
                sp.wait_ge(x_done.sem, x_done.value(i, x_done.per))
                sp.dma_start(out[0:B * L, :].rearrange("(t p) d -> p t d", p=P)[:, bass.ds(i * TILES, TILES), :],
                             x[:, bass.ds(i * TILES, TILES), :]).then_inc(xout, 16)

            with sp.Fori(0, B // PAIR - 1) as i:
                write_out(i)
                for g in range(PAIR):
                    sp.wait_ge(scattered[g].sem, scattered[g].value(i, scattered[g].per))
                    sp.sem_inc(rows_free[g], 1)
            write_out(B // PAIR - 1)
            load_expert(sp, EARLY)
            sp.wait_ge(tables, 2)
            for done_ in scattered:
                sp.wait_ge(done_.sem, B // PAIR * done_.per)

            def load_slot(s):
                row = sp.value_load(slot_row[0:1, bass.ds(s, 1)], min_val=0, max_val=ROWS - P)
                sp.dma_start(xg, routed[bass.ds(row, P), :]).then_inc(xg_loaded, 16)

            def load_next_slot(s):
                sp.wait_ge(xt_done, s)
                sp.wait_ge(wi_out, s)
                load_slot(s)

            load_slot(0)
            load_next_slot(1)
            for e in range(EARLY, X):
                sp.wait_ge(ld_experts, 32 * (e + 1))
                sp.sem_inc(experts_ready, 1)
                if e + 1 < X:
                    load_expert(sp, e + 1)
                load_next_slot(e - EARLY + 2)
            with sp.Fori(X - EARLY + 2, SLOTS) as s:
                load_next_slot(s)

        @block.gpsimd
        def _(pool):
            fill = empty[:, :]
            pool.memset(fill, 0.0).then_inc(const_step, 1)
            pool.wait_ge(const_step, 1)
            pool.iota(fill[:, TOKEN:TOKEN + 1], [[0, 1]], base=B * L, channel_multiplier=1,
                      allow_small_or_imprecise_dtypes=True).then_inc(const_ready, 1)
            pool.memset(ident[:, :], 0.0).then_inc(const_step, 1)
            pool.memset(tri[:, :], 1.0).then_inc(const_step, 1)
            pool.memset(mask[:, :], 1.0).then_inc(const_step, 1)
            pool.memset(ones[:, :], 1.0).then_inc(const_ready, 1)
            pool.memset(quarter[:, :], 0.25).then_inc(const_ready, 1)
            pool.memset(halfneg[:, :], -0.5).then_inc(const_step, 1)
            pool.memset(xnT[:, :, :, 0:1], 0.0).then_inc(const_ready, 1)
            pool.wait_ge(const_step, 5)
            pool.affine_select(out=ident[:, :], in_=ident[:, :], compare_op=ALU.not_equal, fill=1.0, base=0,
                               pattern=[[-1, P]], channel_multiplier=1).then_inc(const_ready, 1)
            pool.affine_select(out=tri[:, :], in_=tri[:, :], compare_op=ALU.is_gt, fill=0.0, base=0,
                               pattern=[[1, P]], channel_multiplier=-1).then_inc(const_ready, 1)
            pool.affine_select(out=mask[:, :], in_=mask[:, :], compare_op=ALU.is_ge, fill=0.0, base=0,
                               pattern=[[-E, G]], channel_multiplier=1).then_inc(const_step, 1)
            pool.wait_ge(const_step, 6)
            pool.affine_select(out=mask[:, :], in_=mask[:, :], compare_op=ALU.is_ge, fill=0.0, base=E - 1,
                               pattern=[[E, G]], channel_multiplier=-1).then_inc(const_step, 1)
            pool.iota(iota8[:, :], [[1, X]], base=0, channel_multiplier=0, allow_small_or_imprecise_dtypes=True).then_inc(const_ready, 1)
            pool.iota(iota8m[:, :], [[1, X]], base=-X, channel_multiplier=0, allow_small_or_imprecise_dtypes=True).then_inc(const_ready, 1)
            pool.iota(region[:, :], [[REGION, X]], base=0, channel_multiplier=0, allow_small_or_imprecise_dtypes=True).then_inc(const_ready, 1)
            pool.iota(iota_s[:, :], [[1, SLOTS]], base=0, channel_multiplier=0, allow_small_or_imprecise_dtypes=True).then_inc(const_ready, 1)
            pool.iota(token[:, :], [[P, NT]], base=0, channel_multiplier=1, allow_small_or_imprecise_dtypes=True).then_inc(const_ready, 1)
            pool.wait_ge(const_step, 7)

            for free in rows_free:
                pool.sem_inc(free, 1)
            for i in range(B // PAIR):
                at = slice(i * TILES, (i + 1) * TILES)
                pool.wait_ge(mv0_ready, (i + 1) * TILES)
                pool.tensor_scalar(rstd0[:, at], mv0[:, at, 1], EPS, None, ALU.add).then_inc(const_step, 1)
                pool.wait_ge(const_step, 8 + i)
                pool.tensor_tensor(rstd0[:, at], rstd0[:, at], halfneg[:, :].to_broadcast([P, TILES]), ALU.pow).then_inc(rstd0_ready, 1)
            pool.wait_ge(keys_out, PRE_KEYS * B)
            with pool.Fori(0, B // PAIR) as i:
                def norm(k, g, j):
                    if k == 0:
                        return
                    t = g * JT + j
                    n = (k - 1) * TILES + t + 1
                    pool.wait_ge(mv_ready.sem, mv_ready.value(i, n))
                    pool.sem_inc(passed, 1)
                    pool.tensor_scalar(veps[:, t:t + 1], mv[:, t, 1:2], EPS, None, ALU.add).then_inc(pool_step.sem, 1)
                    pool.wait_ge(pool_step.sem, pool_step.value(i, n))
                    pool.tensor_tensor(rstd[:, t:t + 1], veps[:, t:t + 1], halfneg[:, :], ALU.pow).then_inc(rstd_ready.sem, 1)

                def block_diagonal_keys(l, g):
                    if l == 1:
                        pool.wait_ge(rg_done.sem, rg_done.value(i, 2 * (g + 1)))
                    for c in range(C):
                        pool.tensor_tensor(
                            kbd[:, g, c, :].rearrange("p (h s) -> p h s", h=G),
                            keys[:, l * C + c, bass.ds((i * PAIR + g) * S, S)].unsqueeze(1).to_broadcast([P, G, S]),
                            mask[:, :].unsqueeze(2).to_broadcast([P, G, S]), ALU.mult).then_inc(kbd_ready.sem, 1)

                def scatter(g, j):
                    if j == 0:
                        pool.wait_ge(packed_done.sem, packed_done.value(i, g + 1))
                        pool.sem_inc(passed, 1)
                        pool.wait_ge(ld_fill, 16)
                    t = g * JT + j
                    for k in range(2):
                        pool.indirect_dma_start(
                            out=routed, out_offset=bass.IndirectOffsetOnAxis(ap=where_[:, k, t:t + 1], axis=0),
                            in_=xn[:, t, :], in_offset=None).then_inc(scattered[g].sem, 16)

                stage_of({"norm": norm, "keys": block_diagonal_keys, "scatter": scatter})

            pool.wait_ge(xout, 16 * (B // PAIR + 1))

            with pool.Fori(0, SLOTS) as s:
                pool.wait_ge(tok_out, s + 1)
                pool.sem_inc(passed, 1)
                pool.indirect_dma_start(out=out, out_offset=bass.IndirectOffsetOnAxis(ap=slot_tok[:, 0:1], axis=0),
                                        in_=ysb[:, :], in_offset=None, compute_op=ALU.add).then_inc(added, 16)
                pool.wait_ge(added, 16 * s + 16)
                pool.sem_inc(ysb_free, 1)

        @block.scalar
        def _(act):
            act.dma_start(cols[:, :], cols_in).then_inc(ld_small, 16)
            act.dma_start(vecs[:, :], vecs_in.rearrange("(p k) -> p k", k=VECW)).then_inc(ld_vecs, 16)
            act.dma_start(wr[:, :, :], wr_in.rearrange("(c p) e -> p c e", p=P)).then_inc(ld_wr, 16)
            act.wait_ge(const_ready, 1)
            act.dma_start(out[B * L:B * L + P, :], empty[:, 0:D]).then_inc(xout, 16)

            act.wait_ge(pre_step, 3)
            for m in range(PRE_VALS):
                act.wait_ge(pre_mm, PRE_KEYS + m + 1)
                for q in range(2):
                    half = slice(q * S, (q + 1) * S)
                    to = vbd[half, m * PAIRS:(m + 1) * PAIRS, q * (E + 1):q * (E + 1) + E]
                    frm = pre_banks[m % PRE_KEYS][half, 0:D].rearrange("s (a q d) -> s a q d", q=2, d=E)[:, :, q, :]
                    act.activation(to, frm, ACT.Copy).then_inc(vals_out, 1)
            act.wait_ge(ld_small, 16)
            act.wait_ge(pre_step, 3 + 2 + 1)
            with act.Fori(0, B // PAIR) as i:
                def copy_turned(n, to, width):
                    act.wait_ge(turned.sem, turned.value(i, n + 1))
                    act.activation(to, ps_t[n % 2][:, 0:width], ACT.Copy).then_inc(turn_read.sem, 1)

                def keep_turned(k, g, h):
                    copy_turned(TURN["turn", k, g, h], xnT[:, g, :, 1 + 2 * h * P:1 + 2 * (h + 1) * P], 2 * D)

                def turn_out(n):
                    copy_turned(TURN["turn_out", n], oT[:, n % 2, :, :], D)

                def queries(l, g):
                    for c in range(C):
                        n = (PAIR * l + g) * C + c + 1
                        act.wait_ge(q_done.sem, q_done.value(i, n))
                        act.activation(qT[:, g, c, :], (ps_w, ps_o)[c][:, :], ACT.Identity,
                                       bias=cols[:, BQ[l] + c:BQ[l] + c + 1]).then_inc(q_out.sem, 1)

                def exp(n):
                    for c in range(C):
                        act.wait_ge(sub_done.sem, sub_done.value(i, n * C + c + 1))
                        if n:
                            act.wait_ge(pt_done.sem, pt_done.value(i, (n - 1) * C + c + 1))
                        act.activation(probs[:, c * 512:(c + 1) * 512], shifted[:, c * 512:(c + 1) * 512],
                                       ACT.Exp).then_inc(exp_done.sem, 1)

                def turn_probs(n):
                    for c in range(C):
                        act.wait_ge(pt_done.sem, pt_done.value(i, n * C + c + 1))
                        if n:
                            act.wait_ge(pv_done.sem, pv_done.value(i, n))
                        act.activation(probsT[:, c * PAIRS // C:(c + 1) * PAIRS // C, :].rearrange("p a t -> p (a t)"),
                                       ps_p[:, c * 512:(c + 1) * 512], ACT.Copy).then_inc(pt_out.sem, 1)

                def before(g, w):
                    act.wait_ge(turn_read.sem, turn_read.value(i, TURN["turn", 1, g, HALVES - 1] + 1))
                    for c in range(C):
                        act.activation(mixed(w, g, c), xnT[:, g, c, 0:L], ACT.Copy,
                                       scale=omu[:, 2 * (1 - w) + c:2 * (1 - w) + c + 1]).then_inc(prev_done.sem, 1)

                def key(g):
                    for c in range(C):
                        act.wait_ge(key_done.sem, key_done.value(i, g * C + c + 1))
                        if c == 0:
                            act.wait_ge(mixk_done.sem, mixk_done.value(i, (g + 1) * C))
                            act.wait_ge(mixr_done.sem, mixr_done.value(i, (g + 1) * C))
                        act.activation(kact(g, c), ps_s[:, c * L:(c + 1) * L], ACT.Relu).then_inc(relu_done.sem, 1)
                    for c in range(C):
                        act.wait_ge(relu_done.sem, relu_done.value(i, g * C + c + 1))
                        act.activation(kact(g, c), kact(g, c), ACT.Square).then_inc(kact_done.sem, 1)

                def gate(g):
                    for half in range(2):
                        act.wait_ge(rg_done.sem, rg_done.value(i, g * 2 + half + 1))
                        act.activation(gate_of(g, half), ps_p[:, half * 512:(half + 1) * 512], ACT.Tanh,
                                       scale=0.5).then_inc(gate_done.sem, 1)

                def logits(g, h):
                    copy_turned(TURN["logits", g, h], r8[:, g, 10, 2 * h:2 * h + 2].rearrange("p t e -> p (t e)"), 2 * X)

                def choose(g, part):
                    if part == 0:
                        act.wait_ge(lsub_done.sem, lsub_done.value(i, g + 1))
                        act.activation(r8[:, g, 1], r8[:, g, 0], ACT.Exp).then_inc(lexp_done.sem, 1)
                    elif part == 3:
                        act.wait_ge(gap_done.sem, gap_done.value(i, g + 1))
                        act.activation(r1[:, g, 7], r1[:, g, 6], ACT.Exp).then_inc(gexp_done.sem, 1)

                def ranked(g):
                    copy_turned(TURN["ranks", g], ranks[:, g].rearrange("p a t e -> p (a t e)"), 2 * JT * X)

                stage_of({"turned": keep_turned, "turn_out": turn_out, "queries": queries, "exp": exp, "turn_probs": turn_probs,
                          "before": before, "key": key, "gate": gate, "logits": logits, "choose": choose,
                          "ranks": ranked})

            def xgT_out(n_done):
                act.wait_ge(xt_done, n_done)
                act.activation(xgT, ps_t[0][:, 0:D].rearrange("p (c t) -> p c t", c=C), ACT.Copy).then_inc(xt_out, 1)

            def gelu(s, first=False):
                e = act.value_load(slot_exp[0:1, bass.ds(s, 1)], min_val=0, max_val=X - 1)
                for k in range(KF):
                    if k % QK == 0:
                        act.wait_ge(hid_done, QUARTERS * s + (k // QK + 1))
                    if not first:
                        act.wait_ge(y_part, KF * s + (k + 1 - KF))
                    act.activation(hidT[:, k, :], hidden_chunk(k), ACT.Gelu,
                                   bias=cols[:, bass.ds(e * KF + (B1 + k), 1)]).then_inc(gelu_done, 1)

            act.wait_ge(tables, 2)
            xgT_out(1)
            gelu(0, first=True)
            xgT_out(2)
            with act.Fori(0, SLOTS - 2) as s:
                xgT_out(s + 3)
                gelu(s + 1)
            gelu(SLOTS - 1)

        @block.tensor
        def _(pe):
            pe.wait_ge(ld_ctx, 16)
            pe.wait_ge(ld_mats[0], 16)
            n = 0
            for l in range(2):
                for c in range(C):
                    bank = pre_banks[n]
                    for k in range(C):
                        mm = pe.matmul(bank[:, 0:B * S], mat(WK[l], k)[:, c * P:(c + 1) * P], ctxT[:, k, :, 0:S],
                                       start=(k == 0), stop=(k == C - 1))
                    mm.then_inc(pre_mm, 1)
                    n += 1
            pe.wait_ge(ld_mats[1], 16)
            pe.wait_ge(const_ready, 5)
            pe.wait_ge(ld_rows3, 48)
            m = 0
            for l in range(2):
                for b in range(B):
                    bank = pre_banks[m % PRE_KEYS]
                    if m < PRE_KEYS:
                        pe.wait_ge(keys_out, B * (m + 1))
                    else:
                        pe.wait_ge(vals_out, 2 * (m - PRE_KEYS + 1))
                    for k in range(C):
                        pe.matmul(bank[:, 0:D], ctxT[:, k, b, :], mat(WV[l], k), start=(k == 0), stop=False)
                    pe.matmul(bank[:, 0:D], ones3, rows3[:, BV[l]:BV[l] + D], start=False, stop=True).then_inc(pre_mm, 1)
                    m += 1
            pe.wait_ge(vals_out, 2 * PRE_VALS)
            pe.wait_ge(ld_mats[2], 16)
            pe.wait_ge(ld_wr, 16)
            with pe.Fori(0, B // PAIR) as i:
                frees = {}

                def wait_free(bank):
                    if bank in frees:
                        signal_, n = frees[bank]
                        pe.wait_ge(signal_.sem, signal_.value(i, n))

                def turn_bank(n):
                    if n >= 2:
                        pe.wait_ge(turn_read.sem, turn_read.value(i, n - 1))
                    return ps_t[n % 2]

                def transposed(n, tiles):
                    bank = turn_bank(n)
                    for c in range(C):
                        for m, tile in enumerate(tiles):
                            at = (c * len(tiles) + m) * P
                            mm = pe.transpose(bank[:, at:at + P], tile[:, c * P:(c + 1) * P], ident[:, :])
                    mm.then_inc(turned.sem, 1)

                def turn(k, g, h):
                    pe.wait_ge(xn_ready.sem, xn_ready.value(i, k * TILES + g * JT + 2 * h + 2))
                    transposed(TURN["turn", k, g, h], [xn[:, g * JT + 2 * h + m, 0:D] for m in range(2)])

                def queries(l, g):
                    pe.wait_ge(turn_read.sem, turn_read.value(i, TURN["turn", 2 * l, g, HALVES - 1] + 1))
                    for c in range(C):
                        n = (PAIR * l + g) * C + c + 1
                        wait_free("wo"[c])
                        for k in range(C):
                            mm = pe.matmul((ps_w, ps_o)[c][:, :], mat(WQ[l], k)[:, c * P:(c + 1) * P],
                                           xnT[:, g, k, 1:L + 1], start=(k == 0), stop=(k == C - 1))
                        mm.then_inc(q_done.sem, 1)
                        frees["wo"[c]] = (q_out, n)

                def scores(n):
                    l, g, j = n // ATT, n % ATT // JT, n % JT
                    if j == 0:
                        pe.wait_ge(q_out.sem, q_out.value(i, (PAIR * l + g + 1) * C))
                        pe.wait_ge(kbd_ready.sem, kbd_ready.value(i, (PAIR * l + g + 1) * C))
                    if n == ATT:
                        pe.wait_ge(relu_done.sem, relu_done.value(i, PAIR * C))
                    for c in range(C):
                        if n:
                            pe.wait_ge(sub_done.sem, sub_done.value(i, (n - 1) * C + c + 1))
                        pe.matmul(ps_s[:, c * 512:(c + 1) * 512], qT[:, g, c, j * P:(j + 1) * P], kbd[:, g, c, :],
                                  start=True, stop=False)
                        pe.matmul(ps_s[:, c * 512:(c + 1) * 512].rearrange("p (h s) -> p h s", h=G), quarter[:, :],
                                  rows3[:, bass.ds((i * PAIR + g) * S + DELTA, S)].unsqueeze(1).to_broadcast([3, G, S]),
                                  start=False, stop=True).then_inc(s_done.sem, 1)

                def turn_probs(n):
                    if n == ATT:
                        pe.wait_ge(gate_done.sem, gate_done.value(i, PAIR * 2))
                    for c in range(C):
                        pe.wait_ge(exp_done.sem, exp_done.value(i, n * C + c + 1))
                        if n:
                            pe.wait_ge(pt_out.sem, pt_out.value(i, (n - 1) * C + c + 1))
                        for a in range(c * PAIRS // C, (c + 1) * PAIRS // C):
                            mm = pe.transpose(ps_p[:, a * P:(a + 1) * P], probs[:, a * P:(a + 1) * P], ident[:, :])
                        mm.then_inc(pt_done.sem, 1)

                def values(n):
                    l, g = n // ATT, n % ATT // JT
                    wait_free("o")
                    for a in range(PAIRS):
                        if a % (PAIRS // C) == 0:
                            pe.wait_ge(pt_out.sem, pt_out.value(i, n * C + a // (PAIRS // C) + 1))
                        mm = pe.matmul(ps_o[:, a * VW:(a + 1) * VW], probsT[:, a, :],
                                       vbd[:, bass.ds((i * PAIR + g) * PAIRS + (l * B * PAIRS + a), 1), :].rearrange("p a w -> p (a w)"),
                                       start=True, stop=True)
                    mm.then_inc(pv_done.sem, 1)
                    frees["o"] = (on_done, n + 1)

                def turn_out(n):
                    pe.wait_ge(on_done.sem, on_done.value(i, n + 1))
                    transposed(TURN["turn_out", n], [onorm])

                def project(n):
                    l = n // ATT
                    pe.wait_ge(turn_read.sem, turn_read.value(i, TURN["turn_out", n] + 1))
                    wait_free("w")
                    for k in range(C):
                        pe.matmul(ps_w[:, 0:D], oT[:, n % 2, k, :], mat(WO[l], k), start=(k == 0), stop=False)
                    pe.matmul(ps_w[:, 0:D], ones3, rows3[:, BO[l]:BO[l] + D], start=False, stop=True).then_inc(pr_done.sem, 1)
                    frees["w"] = (x_done, ADDED["project", n])

                def key(g):
                    pe.wait_ge(mixk_done.sem, mixk_done.value(i, (g + 1) * C))
                    if g == 0:
                        pe.wait_ge(sub_done.sem, sub_done.value(i, ATT * C))
                    else:
                        pe.wait_ge(relu_done.sem, relu_done.value(i, g * C))
                    for c in range(C):
                        for k in range(C):
                            mm = pe.matmul(ps_s[:, c * L:(c + 1) * L], mat(FK, k)[:, c * P:(c + 1) * P], mixed(0, g, k),
                                           start=(k == 0), stop=(k == C - 1))
                        mm.then_inc(key_done.sem, 1)

                def gate(g):
                    pe.wait_ge(mixr_done.sem, mixr_done.value(i, (g + 1) * C))
                    if g == 0:
                        pe.wait_ge(pt_out.sem, pt_out.value(i, ATT * C))
                    else:
                        pe.wait_ge(gate_done.sem, gate_done.value(i, g * 2))
                    for j in range(JT):
                        for k in range(C):
                            mm = pe.matmul(ps_p[:, j * D:(j + 1) * D], mixed(1, g, k)[:, j * P:(j + 1) * P], mat(FR, k),
                                           start=(k == 0), stop=(k == C - 1))
                        if j % 2:
                            mm.then_inc(rg_done.sem, 1)

                def value(g, h):
                    if h == 0:
                        pe.wait_ge(kact_done.sem, kact_done.value(i, (g + 1) * C))
                    for m in range(2):
                        j = 2 * h + m
                        wait_free(VALUE_BANKS[g][m])
                        for k in range(C):
                            mm = pe.matmul(bank_of[VALUE_BANKS[g][m]][:, 0:D], kact(g, k)[:, j * P:(j + 1) * P], mat(FV, k),
                                           start=(k == 0), stop=(k == C - 1))
                        mm.then_inc(val_done.sem, 1)
                        frees[VALUE_BANKS[g][m]] = (gated_done, g * JT + j + 1)

                def logits(g, h):
                    bank = turn_bank(TURN["logits", g, h])
                    pe.wait_ge(turn_read.sem, turn_read.value(i, TURN["turn", 3, g, h] + 1))
                    for m in range(2):
                        t = 2 * h + m
                        to = bank[:, m * X:(m + 1) * X]
                        for k in range(C):
                            pe.matmul(to, xnT[:, g, k, 1 + t * P:1 + (t + 1) * P], wr[:, k, :], start=(k == 0), stop=False)
                        mm = pe.matmul(to, ones3, rows3[:, BR:BR + X], start=False, stop=True)
                    mm.then_inc(turned.sem, 1)

                def ranked(g):
                    bank = turn_bank(TURN["ranks", g])
                    pe.wait_ge(chosen_done.sem, chosen_done.value(i, g + 1))
                    picks = chosen[:, g * JT:(g + 1) * JT, :].rearrange("p t e -> p (t e)")
                    pe.matmul(bank[:, 0:JT * X], tri[:, :], picks, start=True, stop=True)
                    pe.matmul(bank[:, JT * X:2 * JT * X], ones[:, :], picks, start=True, stop=True).then_inc(turned.sem, 1)

                stage_of({"turn": turn, "queries": queries, "scores": scores, "turn_probs": turn_probs, "values": values,
                          "turn_out": turn_out, "project": project, "key": key, "gate": gate, "value": value,
                          "logits": logits, "ranks": ranked})

            def rows_transposed(n_loaded):
                pe.wait_ge(xg_loaded, n_loaded)
                for c in range(C):
                    mm = pe.transpose(ps_t[0][:, c * P:(c + 1) * P], xg[:, c * P:(c + 1) * P], ident[:, :])
                mm.then_inc(xt_done, 1)

            def hidden(s):
                pe.wait_ge(xt_out, s + 1)
                for k in range(KF):
                    if k % QK == 0:
                        pe.wait_ge(w1_ready, QUARTERS * s + (k // QK + 1))
                        if not (isinstance(s, int) and s == 0):
                            pe.wait_ge(gelu_done, KF * s + (k + QK - KF))
                    for c in range(C):
                        mm = pe.matmul(hidden_chunk(k), w1s[:, c, k * P:(k + 1) * P], xgT[:, c, :],
                                       start=(c == 0), stop=(c == C - 1))
                    if k % QK == QK - 1:
                        mm.then_inc(hid_done, 1)

            def result(s):
                e = pe.value_load(slot_exp[0:1, bass.ds(s, 1)], min_val=0, max_val=X - 1)
                pe.wait_ge(ps_y_free, s + 1)
                pe.matmul(ps_w[:, 0:D], ones3, rows3[:, bass.ds(e * D + B2, D)], start=True, stop=False)
                for k in range(KF):
                    pe.wait_ge(gelu_done, KF * s + (k + 1))
                    pe.matmul(ps_w[:, 0:D], hidT[:, k, :], experts[:, bass.ds(e * EW + (C * FF + k * D), D)],
                              start=False, stop=(k == KF - 1)).then_inc(y_part, 1)

            pe.wait_ge(tables, 2)
            rows_transposed(16)
            hidden(0)
            rows_transposed(32)

            def steady(s):
                hidden(s + 1)
                rows_transposed(16 * s + 48)
                result(s)

            with pe.Fori(0, X) as s:
                pe.wait_ge(experts_ready, s + 1)
                steady(s)
            with pe.Fori(X, SLOTS - 2) as s:
                steady(s)
            hidden(SLOTS - 1)
            result(SLOTS - 2)
            result(SLOTS - 1)

        @block.vector
        def _(dve):
            done = [0]

            def step(ins):
                done[0] += 1
                ins.then_inc(pre_step, 1)
                dve.wait_ge(pre_step, done[0])

            dve.memset(vbd[:, :, :], 0.0).then_inc(pre_step, 1)
            done[0] += 1
            dve.wait_ge(pre_step, done[0])
            for q in range(2):
                col = q * (E + 1) + E
                dve.memset(vbd[q * S:(q + 1) * S, :, col:col + 1], 1.0).then_inc(pre_step, 1)
                done[0] += 1
            dve.wait_ge(ld_vecs, 16)
            dve.tensor_copy(vpart[:, 0, :], vecs[:, :]).then_inc(split_ready, 1)
            dve.wait_ge(split_ready, 1)
            step(dve.tensor_tensor(vres[:, 0, :], vecs[:, :], vpart[:, 0, :], ALU.subtract))
            dve.tensor_copy(vpart[:, 1, :], vres[:, 0, :]).then_inc(split_ready, 1)
            dve.wait_ge(split_ready, 2)
            step(dve.tensor_tensor(vres[:, 1, :], vres[:, 0, :], vpart[:, 1, :], ALU.subtract))
            dve.tensor_copy(vpart[:, 2, :], vres[:, 1, :]).then_inc(split_ready, 1)

            dve.wait_ge(ld_small, 16)
            step(dve.tensor_scalar(omu[:, :], cols[:, MU_R:MU_R + 4], -1.0, 1.0, ALU.mult, ALU.add))
            step(dve.tensor_scalar(tau[:, :], cols[:, TAU:TAU + B], 1.0 / E ** 0.5, None, ALU.mult))

            def statistics_of(tiles):
                for t in tiles:
                    dve.bn_stats(fstat0[:, t, :], x[:, t, :]).then_inc(pre_step, 1)
                    done[0] += 1

            def aggregate(i):
                dve.wait_ge(pre_step, done[0])
                for t in range(i * TILES, (i + 1) * TILES):
                    dve.bn_aggr(mv0[:, t, :], fstat0[:, t, :]).then_inc(mv0_ready, 1)

            n = 0
            for l in range(2):
                for c in range(C):
                    dve.wait_ge(pre_mm, n + 1)
                    for b in range(B):
                        dve.tensor_scalar(keys[:, l * C + c, b * S:(b + 1) * S], pre_banks[n][:, b * S:(b + 1) * S],
                                          cols[:, BK[l] + c:BK[l] + c + 1], tau[:, b:b + 1], ALU.add, ALU.mult).then_inc(keys_out, 1)
                    dve.wait_ge(ld_x[0], 16)
                    statistics_of([2 * n, 2 * n + 1])
                    n += 1
            aggregate(0)
            assert TILES == 2 * n
            dve.wait_ge(ld_x[1], 16)
            statistics_of(range(TILES, NT))
            aggregate(1)
            dve.wait_ge(const_ready, 11)
            step(dve.tensor_copy(count[:, :], region[:, :]))

            links = [0]

            def mark(ins):
                links[0] += 1
                ins.then_inc(dve_step.sem, 1)
                return links[0]

            def link(b, ins):
                n = mark(ins)
                dve.wait_ge(dve_step.sem, dve_step.value(b, n))

            with dve.Fori(0, B // PAIR) as i:
                links[0] = 0

                def tile_of(t):
                    return x[:, bass.ds(i * TILES + t, 1), :].rearrange("p t d -> p (t d)")

                def statistics(t):
                    dve.sem_inc(passed, 1)
                    link(i, dve.bn_stats(fstat[:, t, :], tile_of(t)))
                    dve.sem_inc(passed, 1)
                    dve.bn_aggr(mv[:, t, :], fstat[:, t, :]).then_inc(mv_ready.sem, 1)

                def norm(k, g, j):
                    t = g * JT + j
                    if k == 0:
                        dve.wait_ge(rows_free[g], i + 1)
                        dve.wait_ge(rstd0_ready, i + 1)
                        mean, scale = mv0[:, bass.ds(i * TILES + t, 1), 0], rstd0[:, bass.ds(i * TILES + t, 1)]
                    else:
                        n = (k - 1) * TILES + t + 1
                        dve.wait_ge(mv_ready.sem, mv_ready.value(i, n))
                        dve.wait_ge(rstd_ready.sem, rstd_ready.value(i, n))
                        mean, scale = mv[:, t, 0:1], rstd[:, t:t + 1]
                    dve.tensor_scalar(xn[:, t, 0:D], tile_of(t), mean, scale, ALU.subtract, ALU.mult).then_inc(xn_ready.sem, 1)

                def shift(n):
                    for c in range(C):
                        dve.wait_ge(s_done.sem, s_done.value(i, n * C + c + 1))
                        scores = ps_s[:, c * 512:(c + 1) * 512].rearrange("p (h s) -> p h s", h=G)
                        top = smax[:, c * G:(c + 1) * G]
                        link(i, dve.tensor_reduce(top, scores, AX_X, ALU.max))
                        if n:
                            dve.wait_ge(exp_done.sem, exp_done.value(i, (n - 1) * C + c + 1))
                        dve.tensor_tensor(shifted[:, c * 512:(c + 1) * 512].rearrange("p (h s) -> p h s", h=G), scores,
                                          top.unsqueeze(2).to_broadcast([P, G, S]), ALU.subtract).then_inc(sub_done.sem, 1)

                def values(n):
                    dve.wait_ge(pv_done.sem, pv_done.value(i, n + 1))
                    sums = ps_o[:, 0:PAIRS * VW].rearrange("p (h w) -> p h w", h=H)
                    link(i, dve.reciprocal(rsum[:, :], sums[:, :, E]))
                    dve.tensor_tensor(onorm[:, :].rearrange("p (h e) -> p h e", h=H), sums[:, :, 0:E],
                                      rsum[:, :].unsqueeze(2).to_broadcast([P, H, E]), ALU.mult).then_inc(on_done.sem, 1)

                def project(n):
                    t = n % ATT
                    dve.wait_ge(pr_done.sem, pr_done.value(i, n + 1))
                    dve.tensor_tensor(tile_of(t), tile_of(t), ps_w[:, 0:D], ALU.add).then_inc(x_done.sem, 1)
                    dve.wait_ge(x_done.sem, x_done.value(i, ADDED["project", n]))
                    statistics(t)

                def mix(g, w):
                    for c in range(C):
                        dve.wait_ge(prev_done.sem, prev_done.value(i, (g * 2 + w) * C + c + 1))
                        mu = (MU_K, MU_R)[w] + c
                        dve.scalar_tensor_tensor(out=mixed(w, g, c), in0=xnT[:, g, c, 1:L + 1], scalar=cols[:, mu:mu + 1],
                                                 in1=mixed(w, g, c), op0=ALU.mult, op1=ALU.add).then_inc(
                                                     (mixk_done, mixr_done)[w].sem, 1)

                def add(g, h):
                    dve.wait_ge(gate_done.sem, gate_done.value(i, g * 2 + h + 1))
                    tiles = [g * JT + 2 * h + m for m in range(2)]
                    for m, t in enumerate(tiles):
                        dve.wait_ge(val_done.sem, val_done.value(i, t + 1))
                        dve.scalar_tensor_tensor(out=gated[m], in0=gate_of(g, h)[:, m * D:(m + 1) * D], scalar=1.0,
                                                 in1=bank_of[VALUE_BANKS[g][m]][:, 0:D], op0=ALU.add, op1=ALU.mult).then_inc(gated_done.sem, 1)
                    for m, t in enumerate(tiles):
                        dve.wait_ge(gated_done.sem, gated_done.value(i, t + 1))
                        dve.scalar_tensor_tensor(out=tile_of(t), in0=gated[m], scalar=0.5, in1=tile_of(t),
                                                 op0=ALU.mult, op1=ALU.add).then_inc(x_done.sem, 1)
                    for m, t in enumerate(tiles):
                        dve.wait_ge(x_done.sem, x_done.value(i, ADDED["add", g, h] + (m - 1)))
                        dve.sem_inc(passed, 1)
                        n = mark(dve.bn_stats(fstat[:, t, :], tile_of(t)))
                    for m, t in enumerate(tiles):
                        dve.wait_ge(dve_step.sem, dve_step.value(i, n + (m - 1)))
                        dve.sem_inc(passed, 1)
                        dve.bn_aggr(mv[:, t, :], fstat[:, t, :]).then_inc(mv_ready.sem, 1)

                def spread(a):
                    return a.unsqueeze(2).to_broadcast([P, JT, X])

                def along(a):
                    return a.unsqueeze(1).to_broadcast([P, JT, X])

                def pick(g, p, top, first, hot, t1, t2):
                    link(i, dve.tensor_reduce(r1[:, g, top], r8[:, g, p], AX_X, ALU.max))
                    link(i, dve.tensor_tensor(r8[:, g, t1], r8[:, g, p], spread(r1[:, g, top]), ALU.is_equal))
                    link(i, dve.scalar_tensor_tensor(out=r8[:, g, t2], in0=r8[:, g, t1], scalar=float(-X),
                                                     in1=along(iota8[:, :]), op0=ALU.mult, op1=ALU.add))
                    link(i, dve.tensor_reduce(r1[:, g, first], r8[:, g, t2], AX_X, ALU.min))
                    link(i, dve.tensor_tensor(r8[:, g, hot], along(iota8m[:, :]), spread(r1[:, g, first]), ALU.is_equal))

                def choose(g, part):
                    mine = slice(g * JT, (g + 1) * JT)
                    if part == 0:
                        dve.wait_ge(turn_read.sem, turn_read.value(i, TURN["logits", g, HALVES - 1] + 1))
                        link(i, dve.tensor_reduce(r1[:, g, 0], r8[:, g, 10], AX_X, ALU.max))
                        dve.tensor_tensor(r8[:, g, 0], r8[:, g, 10], spread(r1[:, g, 0]), ALU.subtract).then_inc(lsub_done.sem, 1)
                    elif part == 1:
                        dve.wait_ge(lexp_done.sem, lexp_done.value(i, g + 1))
                        link(i, dve.tensor_reduce(r1[:, g, 1], r8[:, g, 1], AX_X, ALU.add))
                        link(i, dve.reciprocal(r1[:, g, 2], r1[:, g, 1]))
                        link(i, dve.tensor_tensor(r8[:, g, 2], r8[:, g, 1], spread(r1[:, g, 2]), ALU.mult))
                        pick(g, 2, 3, 4, 3, 4, 5)
                        link(i, dve.scalar_tensor_tensor(out=r8[:, g, 6], in0=r8[:, g, 3], scalar=-2.0, in1=r8[:, g, 2],
                                                         op0=ALU.mult, op1=ALU.add))
                    elif part == 2:
                        pick(g, 6, 5, 8, 7, 4, 5)
                        dve.tensor_tensor(chosen[:, mine, :], r8[:, g, 3], r8[:, g, 7], ALU.add).then_inc(chosen_done.sem, 1)
                        dve.tensor_tensor(r1[:, g, 6], r1[:, g, 5], r1[:, g, 3], ALU.subtract).then_inc(gap_done.sem, 1)
                    else:
                        mark(dve.tensor_scalar(xn[:, mine, FIRST], r1[:, g, 4], float(X), None, ALU.add))
                        mark(dve.tensor_copy(xn[:, mine, TOKEN], token[:, bass.ds(i * TILES + g * JT, JT)]))
                        dve.wait_ge(gexp_done.sem, gexp_done.value(i, g + 1))
                        link(i, dve.tensor_scalar(r1[:, g, 8], r1[:, g, 7], 1.0, None, ALU.add))
                        link(i, dve.reciprocal(r1[:, g, 9], r1[:, g, 8]))
                        mark(dve.tensor_copy(xn[:, mine, W1ST], r1[:, g, 9]))
                        mark(dve.tensor_tensor(xn[:, mine, W2ND], r1[:, g, 9], r1[:, g, 7], ALU.mult))

                def places(g):
                    dve.wait_ge(turn_read.sem, turn_read.value(i, TURN["ranks", g] + 1))
                    for t in range(JT):
                        mark(dve.tensor_tensor(r8[:, g, 8, t], ranks[:, g, 0, t], count[:, :], ALU.add))
                        link(i, dve.tensor_tensor(count[:, :], ranks[:, g, 1, t], count[:, :], ALU.add))
                    link(i, dve.tensor_tensor(r8[:, g, 4:6], r8[:, g, 8].unsqueeze(1).to_broadcast([P, 2, JT, X]),
                                              r8[:, g, 3:8:4], ALU.mult))
                    link(i, dve.tensor_reduce(r1[:, g, 3:5], r8[:, g, 4:6], AX_X, ALU.add))
                    link(i, dve.tensor_copy(where_[:, :, g * JT:(g + 1) * JT], r1[:, g, 3:5]))
                    dve.sem_inc(packed_done.sem, 1)

                stage_of({"norm": norm, "shift": shift, "values": values, "project": project,
                          "mix": mix, "add": add, "choose": choose, "places": places})
                assert links[0] == DVE_STEPS, links[0]

            done[0] = 0

            def tstep(ins):
                done[0] += 1
                ins.then_inc(tab_step, 1)
                dve.wait_ge(tab_step, done[0])

            def over_slots(a):
                return a.unsqueeze(1).to_broadcast([P, SLOTS, X])

            tstep(dve.scalar_tensor_tensor(out=tt[:, 0, :], in0=count[:, :], scalar=float(P - 1), in1=region[:, :],
                                           op0=ALU.add, op1=ALU.subtract))
            tstep(dve.tensor_copy(tti[:, :], tt[:, 0, :]))
            tstep(dve.tensor_scalar(tti[:, :], tti[:, :], P.bit_length() - 1, None, ALU.logical_shift_right))
            tstep(dve.tensor_copy(tt[:, 1, :], tti[:, :]))
            tstep(dve.tensor_scalar(tt[:, 1, :], tt[:, 1, :], 1.0, None, ALU.max))
            tstep(dve.memset(tt[:, 2, :], 1.0))
            tstep(dve.tensor_tensor_scan(tt[:, 3, :], tt[:, 2, :], tt[:, 1, :], 0.0, ALU.mult, ALU.add))
            tstep(dve.tensor_tensor(ge, iota_s[:, :].unsqueeze(2).to_broadcast([P, SLOTS, X]),
                                    over_slots(tt[:, 3, :]), ALU.is_ge))
            tstep(dve.tensor_reduce(st[:, 0, :], ge, AX_X, ALU.add))
            tstep(dve.tensor_tensor(gen, ge, over_slots(tt[:, 1, :]), ALU.mult))
            tstep(dve.tensor_reduce(st[:, 1, :], gen, AX_X, ALU.add))
            tstep(dve.tensor_tensor(st[:, 2, :], iota_s[:, :], st[:, 1, :], ALU.subtract))
            tstep(dve.scalar_tensor_tensor(out=st[:, 3, :], in0=st[:, 0, :], scalar=float(REGION // P), in1=st[:, 2, :],
                                           op0=ALU.mult, op1=ALU.add))
            tstep(dve.tensor_scalar(st[:, 4, :], st[:, 0, :], float(X - 1), None, ALU.min))
            dve.tensor_scalar(slot_row[:, :], st[0:1, 3, :], float(P), None, ALU.mult).then_inc(tables, 1)
            dve.tensor_copy(slot_exp[:, :], st[0:1, 4, :]).then_inc(tables, 1)
            dve.sem_inc(ps_y_free, 1)
            dve.sem_inc(ysb_free, 1)

            def column(a, s, k):
                return a[:, bass.ds(s, 1), k:k + 1].rearrange("p s w -> p (s w)")

            def take(s, n_loaded):
                dve.wait_ge(xg_loaded, n_loaded)
                dve.tensor_copy(slot_cols[:, bass.ds(s, 1), :].rearrange("p s w -> p (s w)"),
                                xg[:, D:RW]).then_inc(wi_out, 1)

            def copy_first_matrix(s):
                e = dve.value_load(slot_exp[0:1, bass.ds(s, 1)], min_val=0, max_val=X - 1)
                for q in range(QUARTERS):
                    if not (isinstance(s, int) and s == 0):
                        dve.wait_ge(hid_done, QUARTERS * s + (q + 1 - QUARTERS))
                    at = q * QK * P
                    frm = experts[:, bass.ds(e * EW, C * FF)].rearrange("p (c f) -> p c f", c=C)
                    dve.tensor_copy(w1s[:, :, at:at + QK * P], frm[:, :, at:at + QK * P]).then_inc(w1_ready, 1)

            TABS = done[0]
            SLOT_STEPS = 4

            def weigh(s):
                dve.wait_ge(wi_out, s + 1)
                expert = st[:, 4, bass.ds(s, 1)]
                for k, (col, test) in enumerate([(0, ALU.is_equal), (1, ALU.not_equal)]):
                    dve.tensor_scalar(column(slot_w, s, k), column(slot_cols, s, FIRST - D), expert,
                                      column(slot_cols, s, col), test, ALU.mult).then_inc(tab_step, 1)
                dve.wait_ge(tab_step, SLOT_STEPS * s + (TABS + 2))
                dve.tensor_tensor(column(slot_w, s, 2), column(slot_w, s, 0), column(slot_w, s, 1), ALU.add).then_inc(tab_step, 1)
                dve.wait_ge(ysb_free, s + 1)
                dve.tensor_copy(slot_tok[:, :], column(slot_cols, s, TOKEN - D)).then_inc(tab_step, 1)
                dve.wait_ge(tab_step, SLOT_STEPS * s + (TABS + 4))
                dve.wait_ge(y_part, KF * s + KF)
                dve.tensor_scalar(ysb[:, :], ps_w[:, 0:D], column(slot_w, s, 2), None, ALU.mult).then_inc(ps_y_free, 1)
                dve.wait_ge(ps_y_free, s + 2)
                dve.sem_inc(tok_out, 1)

            dve.wait_ge(tables, 2)
            dve.wait_ge(xout, 16 * (B // PAIR + 1))
            dve.wait_ge(experts_ready, 2)
            copy_first_matrix(0)
            take(0, 16)
            copy_first_matrix(1)
            take(1, 32)

            def steady(s):
                take(s + 2, 16 * s + 48)
                copy_first_matrix(s + 2)
                weigh(s)

            with dve.Fori(0, X - 2) as s:
                dve.wait_ge(experts_ready, s + 3)
                steady(s)
            with dve.Fori(X - 2, SLOTS - 2) as s:
                steady(s)
            weigh(SLOTS - 2)
            weigh(SLOTS - 1)


def kernel(**inputs):
    import numpy as np
    import concourse.bacc as bacc
    from concourse.bass_utils import run_bass_kernel_spmd

    def get(name):
        return np.ascontiguousarray(inputs[name])

    ctx = get("ctx_1024").transpose(2, 0, 1)
    ctx = np.ascontiguousarray(np.concatenate([ctx, ctx], axis=2)).reshape(D, B * 2 * S)
    names = ["L0_xcond_Wk", "L1_xcond_Wk", "L0_xcond_Wv", "L1_xcond_Wv", "L0_xcond_Wq", "L1_xcond_Wq", "L0_xcond_Wo",
             "L1_xcond_Wo", "L0_ffn_W_r", "L0_ffn_W_k", "L0_ffn_W_v"]
    mats = np.ascontiguousarray(np.stack([get(n).T for n in names]))
    by_col = ["L0_xcond_bq", "L0_xcond_bk", "L1_xcond_bq", "L1_xcond_bk", "L0_ffn_mu_r", "L0_ffn_mu_k", "L1_ffn_b1"]
    cols = np.concatenate([get(n).reshape(-1, P) for n in by_col]).T
    cols = np.ascontiguousarray(np.concatenate([cols, np.broadcast_to(get("condB_tau"), (P, B))], axis=1))
    by_row = ["fside_BxS2_0", "L0_xcond_bo", "L1_xcond_bo", "L0_xcond_bv", "L1_xcond_bv", "L1_ffn_b2", "L1_ffn_br"]
    vecs = np.concatenate([get(n).reshape(-1) for n in by_row])
    vecs = np.concatenate([vecs, np.zeros(VECS - vecs.size, vecs.dtype)])
    arrays = {
        "in_x": get("x").reshape(B * L, D), "in_ctx": ctx, "in_mats": mats, "in_cols": cols,
        "in_vecs": vecs, "in_w1": get("L1_ffn_W1"), "in_w2": get("L1_ffn_W2"), "in_wr": get("L1_ffn_Wr"),
    }
    nc = bacc.Bacc("TRN2", target_bir_lowering=False, num_devices=1)
    args = [nc.dram_tensor(n, a.shape, mybir.dt.from_np(a.dtype), kind="ExternalInput").ap() for n, a in arrays.items()]
    args.append(nc.dram_tensor("out_x", (B * L + P, D), F32, kind="ExternalOutput").ap())
    build(nc, *args)
    r = run_bass_kernel_spmd(nc, [arrays], core_ids=[0])
    return r.results[0]["out_x"][0:B * L].reshape(B, L, D)
```
